# Optimizing a Trainium2 kernel written in Bass

```python
import numpy as np
import jax
import jax.numpy as jnp

def _softmax(x, axis=-1):
    return jax.nn.softmax(x, axis=axis)

def _gelu(x):
    return jax.nn.gelu(x, approximate=True)

def _silu(x):
    return jax.nn.silu(x)

def _sigmoid(x):
    return jax.nn.sigmoid(x)

def _layernorm(x, axis=-1, eps=1e-05):
    m = jnp.mean(x, axis=axis, keepdims=True)
    v = jnp.var(x, axis=axis, keepdims=True)
    return (x - m) / jnp.sqrt(v + eps)

def _scatter_add(tgt, idx, src, axis=0):
    return tgt.at[idx].add(src)

def _segment_sum(src, seg, n):
    return jax.ops.segment_sum(src, seg, n)
kernel_name = 'mk_adj_resnorm_d2_adj_r2_eb8da8'

def setup_inputs(seed: int=0):
    np.random.seed(seed)
    _w = jnp.asarray

    def _rec_inputs():
        import jax
        import jax.numpy as jnp
        _gk = jax.random.key(seed)
        x = 0.0001732 + 1 * jax.random.normal(jax.random.fold_in(_gk, 1), (5120, 64), jnp.float32)
        _a = jax.random.bernoulli(jax.random.fold_in(_gk, 2), 0.0015625, (5120, 5120))
        _af = _a.astype(jnp.float32)
        _af = _af * jax.random.uniform(jax.random.fold_in(_gk, 3), (5120, 5120), jnp.float32, 0.05, 0.02)
        adj = _af
        return (x, adj)
    x, adj = _rec_inputs()

    def _L0_gnn_setup():
        import jax, jax.numpy as jnp
        import numpy as np
        N_USERS = 2048
        N_ITEMS = 3072
        EMB = 64
        LN_EPS = 1e-05
        key = jax.random.key(seed)
        ks = jax.random.split(key, 10)
        N = N_USERS + N_ITEMS
        ego = jax.random.normal(ks[0], (N, EMB), jnp.float32)
        adj = (jax.random.uniform(ks[1], (N, N), jnp.float32) < 0.01).astype(jnp.float32) * 0.02
        xav = float(np.sqrt(6.0 / (EMB + EMB)))
        W_u = jax.random.uniform(ks[2], (EMB, EMB), jnp.float32, -xav, xav)
        W_i = jax.random.uniform(ks[3], (EMB, EMB), jnp.float32, -xav, xav)
        diag_u = jax.random.uniform(ks[4], (N_USERS,), jnp.float32, 0.99, 1.01)
        diag_i = jax.random.uniform(ks[5], (N_ITEMS,), jnp.float32, 0.99, 1.01)
        par_u = jax.random.uniform(ks[6], (2,), jnp.float32, 0.0, 0.99)
        par_i = jax.random.uniform(ks[7], (2,), jnp.float32, 0.0, 0.99)
        ln_gamma = jnp.ones((EMB,), jnp.float32)
        ln_beta = jnp.zeros((EMB,), jnp.float32)
        return {'ego_embeddings': ego, 'adj': adj, 'W_u': W_u, 'diag_u': diag_u, 'par_u': par_u, 'W_i': W_i, 'diag_i': diag_i, 'par_i': par_i, 'ln_gamma': ln_gamma, 'ln_beta': ln_beta}
    _L0_gnn_all = _L0_gnn_setup()
    _L0_gnn_in = {k: v for k, v in _L0_gnn_all.items() if k in ('W_u', 'diag_u', 'par_u', 'W_i', 'diag_i', 'par_i', 'ln_gamma', 'ln_beta')}
    del _L0_gnn_all

    def _L1_gnn_setup():
        import jax, jax.numpy as jnp
        import numpy as np
        N, IN_F, OUT_F, K = (8192, 64, 64, 4)
        key = jax.random.key(seed)
        k1, k2, k3 = jax.random.split(key, 3)
        x = jax.random.normal(k1, (N, IN_F), dtype=jnp.float32)
        L_scaled = jax.random.normal(k2, (N, N), dtype=jnp.float32) / np.sqrt(N)
        fan_in, fan_out = (K * IN_F, OUT_F)
        bound = np.sqrt(6.0 / (fan_in + fan_out))
        weight = jax.random.uniform(k3, (K, IN_F, OUT_F), dtype=jnp.float32, minval=-bound, maxval=bound)
        bias = jnp.zeros((OUT_F,), dtype=jnp.float32)
        return {'x': x, 'L_scaled': L_scaled, 'weight': weight, 'bias': bias}
    _L1_gnn_all = _L1_gnn_setup()
    _L1_gnn_in = {k: v for k, v in _L1_gnn_all.items() if k in ('weight', 'bias')}
    del _L1_gnn_all
    return {'x': x, 'adj': adj, 'L0_gnn_W_u': _L0_gnn_in['W_u'], 'L0_gnn_diag_u': _L0_gnn_in['diag_u'], 'L0_gnn_par_u': _L0_gnn_in['par_u'], 'L0_gnn_W_i': _L0_gnn_in['W_i'], 'L0_gnn_diag_i': _L0_gnn_in['diag_i'], 'L0_gnn_par_i': _L0_gnn_in['par_i'], 'L0_gnn_ln_gamma': _L0_gnn_in['ln_gamma'], 'L0_gnn_ln_beta': _L0_gnn_in['ln_beta'], 'L1_gnn_weight': _L1_gnn_in['weight'], 'L1_gnn_bias': _L1_gnn_in['bias']}

def reference(x, adj, L0_gnn_W_u, L0_gnn_diag_u, L0_gnn_par_u, L0_gnn_W_i, L0_gnn_diag_i, L0_gnn_par_i, L0_gnn_ln_gamma, L0_gnn_ln_beta, L1_gnn_weight, L1_gnn_bias):
    import jax
    import jax.numpy as jnp

    def _L0_gnn_ref(ego_embeddings, adj, W_u, diag_u, par_u, W_i, diag_i, par_i, ln_gamma, ln_beta):
        import jax, jax.numpy as jnp
        import numpy as np
        N_USERS = 2048
        N_ITEMS = 3072
        EMB = 64
        LN_EPS = 1e-05
        nu = diag_u.shape[0]
        res = ego_embeddings
        ego_u = ego_embeddings[:nu]
        ego_i = ego_embeddings[nu:]
        u = par_u[0] * par_u[1] * (diag_u[:, None] * ego_u @ W_u) + ego_u
        i = par_i[0] * par_i[1] * (diag_i[:, None] * ego_i @ W_i) + ego_i
        e = jnp.concatenate([u, i], axis=0)
        h = adj @ (adj.T @ e)
        mu = jnp.mean(h, axis=-1, keepdims=True)
        var = jnp.var(h, axis=-1, keepdims=True)
        out = (h - mu) * jax.lax.rsqrt(var + LN_EPS) * ln_gamma + ln_beta + res
        return out

    def _L1_gnn_ref(x, L_scaled, weight, bias):
        import jax, jax.numpy as jnp
        import numpy as np
        N, IN_F, OUT_F, K = (8192, 64, 64, 4)
        Tx_prev2 = x
        Tx_prev1 = L_scaled @ x
        out = Tx_prev2 @ weight[0]
        if K > 1:
            out = out + Tx_prev1 @ weight[1]
        for k in range(2, K):
            Tx_curr = 2.0 * (L_scaled @ Tx_prev1) - Tx_prev2
            out = out + Tx_curr @ weight[k]
            Tx_prev2, Tx_prev1 = (Tx_prev1, Tx_curr)
        return out + bias
    x = _layernorm(x + _L0_gnn_ref(x, adj, L0_gnn_W_u, L0_gnn_diag_u, L0_gnn_par_u, L0_gnn_W_i, L0_gnn_diag_i, L0_gnn_par_i, L0_gnn_ln_gamma, L0_gnn_ln_beta), axis=-1)
    x = _layernorm(x + _L1_gnn_ref(x, adj, L1_gnn_weight, L1_gnn_bias), axis=-1)
    return x

_drawn_inputs = setup_inputs


def setup_inputs(seed=0):
    import zlib

    import numpy as np

    out = dict(_drawn_inputs(seed))
    spreads = {'L0_gnn_ln_gamma': (1.0, 0.2), 'L0_gnn_ln_beta': (0.0, 0.1), 'L1_gnn_bias': (0.0, 0.1)}
    factors = {'L0_gnn_diag_u': 8.0, 'L0_gnn_W_i': 6.213, 'L0_gnn_diag_i': 8.0}
    for name, (base, spread) in spreads.items():
        noise = np.random.default_rng([zlib.crc32(name.encode()), seed]).standard_normal(out[name].shape)
        drawn = base * np.exp(spread * noise) if base else spread * noise
        out[name] = jnp.asarray(drawn.astype(out[name].dtype))
    for name, factor in factors.items():
        out[name] = (out[name] * factor).astype(out[name].dtype)
    return out
```

```python
from contextlib import ExitStack

import concourse.bass as bass
from concourse import mybir

F32 = mybir.dt.float32
BF16 = mybir.dt.bfloat16
ALU = mybir.AluOpType
ACT = mybir.ActivationFunctionType
AX = mybir.AxisListType.X

P = 128
H = 64
PH = 2 * H
Q32 = 32
BANK = 512
PW = 256
PB = PW // P
NQ = P // Q32
EPS = 1e-5
RAW = 4
TURNED = 2
DMA = 16


def resnorm_chebyshev(nc, x, adj, W_u, diag_u, par_u, W_i, diag_i, par_i, gamma, beta, weight, bias, out):
    N = adj.shape[0]
    NU = diag_u.shape[0]
    NB = N // P
    NG = N // BANK
    NJ = N // PW
    GB = BANK // P
    NS = NG // 2
    SB = 2 * GB
    UB = NU // P
    assert x.shape[1] == H and N % (2 * BANK) == 0 and NU % P == 0 and NG % 2 == 0 and NJ % 2 == 0
    assert (2 * NG) % RAW == 0 and (2 * NG) % TURNED == 0

    with ExitStack() as ctx:
        def sb(name, shape, dt=F32):
            return ctx.enter_context(nc.sbuf_tensor(name, shape, dt))

        def sem(name):
            return ctx.enter_context(nc.semaphore(name))

        panel_size = NB * PW
        shared = sb("shared", [P, 2 * panel_size + NB * H + 2 * PB * BANK])
        panels = [shared[:, k * panel_size:(k + 1) * panel_size].rearrange("p (b c) -> p b c", c=PW)
                  for k in range(2)]
        at = 2 * panel_size
        e = shared[:, at:at + NB * H].rearrange("p (b f) -> p b f", f=H)
        at += NB * H
        at_turned = [[shared[:, at + (2 * cc + gg) * BANK:at + (2 * cc + gg + 1) * BANK] for gg in range(2)]
                     for cc in range(PB)]
        sums1 = shared[:, 0:N]
        sums2 = shared[:, N:2 * N]
        p_turned = shared[0:H, 2 * N + NB * H:2 * N + NB * H + BANK]
        r_start = shared[:, 2 * N:2 * N + NB * H].rearrange("p (k f) -> p k f", f=H)

        terms = sb("terms", [P, NB, 3 * H])
        xq = sb("xq", [P, NB, H])
        raw = sb("raw", [P, RAW, GB * BANK])
        turned = sb("turned", [P, TURNED, GB * BANK])
        ident = sb("ident", [P, P])
        both = sb("both", [P, H])
        zeros = sb("zeros", [P, BANK], BF16)
        t_sum = sb("t_sum", [P, PW])
        t_cols = sb("t_cols", [P, 2, PB * H])
        scratch = sb("scratch", [P, 4, BANK])
        squares = sb("squares", [P, BANK])
        stats = sb("stats", [P, 8, 2 * GB])
        wu = sb("wu", [H, H])
        wi = sb("wi", [H, H])
        par = sb("par", [H, 4])
        scales = sb("scales", [H, 2])
        diag_rows = sb("diag_rows", [NB, P])
        diag = sb("diag", [P, NB])
        w = sb("w", [P, 4, H])
        w_sums1 = sb("w_sums1", [P, H])
        w_sums2 = sb("w_sums2", [P, H])
        w_sums3 = sb("w_sums3", [P, H])
        w_p = sb("w_p", [H, H])
        rows = sb("rows", [P, 3, H])

        banks = [ctx.enter_context(nc.psum_tensor(f"bank{i}", [P, BANK], F32)) for i in range(8)]
        h_bank = banks[0:NS]
        t_bank = banks[5]
        turn_bank = banks[6:8]
        sum_bank = banks[6:8]
        back_bank = banks[5]
        pt_bank = banks[4]
        out_bank = banks[2:4]

        consts_loaded = sem("consts_loaded")
        x_loaded = sem("x_loaded")
        xq_loaded = sem("xq_loaded")
        xq_made = sem("xq_made")
        late_loaded = sem("late_loaded")
        zeroed = sem("zeroed")
        ident_made = sem("ident_made")
        diag_turned = sem("diag_turned")
        x_scaled = sem("x_scaled")
        x_turned = sem("x_turned")
        x_copied = sem("x_copied")
        e_product = sem("e_product")
        e_made = sem("e_made")
        seg_loaded = [[sem(f"seg_loaded{k}_{s}") for s in range(NS)] for k in range(2)]
        seg_done = sem("seg_done")
        at_made = [sem(f"at_made{gg}") for gg in range(2)]
        at_copied = [sem(f"at_copied{gg}") for gg in range(2)]
        at_used = [sem(f"at_used{gg}") for gg in range(2)]
        t_summed = sem("t_summed")
        t_copied = sem("t_copied")
        t_combined = sem("t_combined")
        t_ready = sem("t_ready")
        h_copied = sem("h_copied")
        h_turned = sem("h_turned")
        y_copied = sem("y_copied")
        normed = sem("normed")
        dve_step = sem("dve_step")
        pool_step = sem("pool_step")
        var_made = sem("var_made")
        root_made = sem("root_made")
        raw_loaded = [sem(f"raw_loaded{k}") for k in range(RAW)]
        tile_turned = sem("tile_turned")
        tile_used = sem("tile_used")
        row_copied = sem("row_copied")
        row_kept = sem("row_kept")
        row_back = sem("row_back")
        row_written = sem("row_written")
        weights_made = sem("weights_made")
        pt_turned = sem("pt_turned")
        pt_copied = sem("pt_copied")
        out_summed = sem("out_summed")
        out_taken = sem("out_taken")
        out_made = sem("out_made")
        out_stored = [sem(f"out_stored{k}") for k in range(2)]

        SEGS = [NS - 1 - k for k in range(NS)]
        DOWN = [NG - 1 - k for k in range(NG)]

        sweep2 = [(g, c) for g in DOWN for c in [*range(NG - 1, g + 1, -1), g, *([g + 1] if g + 1 < NG else [])]]
        sweep3 = [(g, c) for g in DOWN for c in range(g, -1, -1)]
        T2 = NG * NG
        late_tiles = sweep2 + sweep3
        row_end = {n: (n + 1) * NG for n in range(NG)}
        for n in range(NG, 3 * NG):
            row_end[n] = row_end[n - 1] + (n - NG + 1 if n < 2 * NG else 3 * NG - n)
        PAIR = 2 * NG

        ROWS1, ROWS2 = NG, 2 * NG

        def by_chunk(a, width):
            return a.rearrange("p (k f) -> p k f", f=width)

        def wide(a, count):
            return a.rearrange("p (k o) -> p k o", o=1).to_broadcast([P, count, H])

        def quarter(a, g, q):
            return a[BANK * g + P * q:BANK * g + P * (q + 1), :].rearrange("(c j) f -> j c f", j=Q32)

        def chunk_order(a):
            return a.rearrange("p (q c j) -> p c q j", q=NQ, j=Q32)

        def split(a):
            return a.rearrange("p (c q j) -> p c q j", q=NQ, j=Q32)

        block = ctx.enter_context(nc.Block())

        @block.sync
        def _(sp):
            sp.dma_start(diag_rows[0:UB, :], diag_u.rearrange("(b p) -> b p", p=P)).then_inc(consts_loaded, DMA)
            sp.dma_start(diag_rows[UB:NB, :], diag_i.rearrange("(b p) -> b p", p=P)).then_inc(consts_loaded, DMA)
            sp.dma_start(e[:, :, :], x.rearrange("(b p) f -> p b f", p=P)).then_inc(x_loaded, DMA)
            sp.dma_start(wu[:, :], W_u).then_inc(consts_loaded, DMA)
            sp.dma_start(wi[:, :], W_i).then_inc(consts_loaded, DMA)
            for k, a in enumerate((par_u, par_i)):
                sp.dma_start(par[:, 2 * k:2 * k + 2], a.rearrange("(o n) -> o n", o=1).to_broadcast([H, 2]))\
                    .then_inc(consts_loaded, DMA)

            seg_rows = adj.rearrange("(s b p) c -> s p b c", p=P, b=SB)
            with sp.Fori(1, NJ // 2 + 1) as pair:
                end = sp.snap(pair * (2 * PW))
                for slot in range(2):
                    for k, s in enumerate(SEGS):
                        sp.wait_ge(seg_done, pair * (2 * NS) + ((slot - 2) * NS + k + 1))
                        sp.dma_start(panels[slot][:, s * SB:(s + 1) * SB, :],
                                     seg_rows[s][:, :, bass.ds(end + (slot - 2) * PW, PW)])\
                            .then_inc(seg_loaded[slot][s], DMA)

            block_rows = adj.rearrange("(b i) c -> i b c", i=Q32)

            def load_tile(slot, t, first_block, column):
                sp.wait_ge(tile_turned, t + 1)
                for q in reversed(range(NQ)):
                    sp.dma_start(raw[Q32 * q:Q32 * (q + 1), slot, :].rearrange("p (b c) -> p b c", c=P),
                                 block_rows[:, bass.ds(first_block, BANK // Q32), column + P * q:column + P * (q + 1)])\
                        .then_inc(raw_loaded[slot], DMA)

            with sp.Fori(0, NG // 2) as two:
                for n in range(PAIR):
                    load_tile(n % RAW, two * PAIR + n, (two * 2 + n // NG) * (BANK // Q32), DOWN[n % NG] * BANK)
            for n, (g, c) in enumerate(late_tiles):
                load_tile((T2 + n) % RAW, T2 + n, g * (BANK // Q32), c * BANK)

        @block.gpsimd
        def _(pool):
            nc.gpsimd.memset(ident[:, :], 0.0).then_inc(pool_step, 1)
            nc.gpsimd.memset(both[:, :], 0.0).then_inc(pool_step, 1)
            pool.wait_ge(pool_step, 2)
            nc.gpsimd.affine_select(out=ident[:, :], in_=ident[:, :], compare_op=ALU.not_equal, fill=1.0,
                                    base=0, pattern=[[-1, P]], channel_multiplier=1).then_inc(ident_made, 1)
            nc.gpsimd.affine_select(out=both[:, :], in_=both[:, :], compare_op=ALU.not_equal, fill=1.0,
                                    base=0, pattern=[[-1, H]], channel_multiplier=1).then_inc(pool_step, 1)
            pool.wait_ge(pool_step, 3)
            nc.gpsimd.affine_select(out=both[:, :], in_=both[:, :], compare_op=ALU.not_equal, fill=1.0,
                                    base=-H, pattern=[[-1, H]], channel_multiplier=1).then_inc(ident_made, 1)
            for k, a in enumerate((gamma, beta, bias)):
                pool.dma_start(rows[:, k, :], a.rearrange("(o f) -> o f", o=1).to_broadcast([P, H]))\
                    .then_inc(late_loaded, DMA)
            for k in range(2):
                pool.dma_start(w[H * k:H * (k + 1), :, :], weight.rearrange("k i o -> i k o"))\
                    .then_inc(late_loaded, DMA)
            for g in range(NG):
                for q in range(NQ):
                    pool.dma_start(xq[Q32 * q:Q32 * (q + 1), g * GB:(g + 1) * GB, :], quarter(x, g, q))\
                        .then_inc(xq_loaded, DMA)
            nc.gpsimd.memset(zeros[:, :], 0.0).then_inc(zeroed, 1)
            nc.gpsimd.memset(terms[:, :, H:3 * H], 0.0).then_inc(zeroed, 1)
            pool.wait_ge(late_loaded, DMA * 5)
            pool.wait_ge(xq_loaded, DMA * NG * NQ)
            nc.gpsimd.tensor_tensor(out=xq[:, :, :], in0=xq[:, :, :], in1=xq[:, :, :], op=ALU.add)\
                .then_inc(pool_step, 1)
            pool.wait_ge(pool_step, 4)
            nc.gpsimd.tensor_tensor(out=xq[:, :, :], in0=xq[:, :, :],
                                    in1=rows[:, 1:2, :].to_broadcast([P, NB, H]), op=ALU.add).then_inc(xq_made, 1)
            for n, g in enumerate(DOWN):
                pool.wait_ge(out_made, n + 1)
                for q in range(NQ):
                    pool.dma_start(quarter(out, g, q), by_chunk(scratch[Q32 * q:Q32 * (q + 1), 2 + n % 2, 0:GB * H], H))\
                        .then_inc(out_stored[n % 2], DMA)
            for k in range(2):
                pool.wait_ge(out_stored[k], DMA * NQ * (NG // 2))

        @block.vector
        def _(dve):
            steps = [0]

            def chain(instruction):
                steps[0] += 1
                instruction.then_inc(dve_step, 1)
                dve.wait_ge(dve_step, steps[0])

            roots = [0]

            def center(y, sq, count):
                s1, s2, inv = (stats[:, i, 0:count] for i in range(3))
                roots[0] += 1
                chain(nc.vector.tensor_reduce(out=s1, in_=y, axis=AX, op=ALU.add))
                chain(nc.vector.tensor_scalar(s1, s1, 1.0 / H, None, ALU.mult))
                chain(nc.vector.tensor_tensor(y, y, wide(s1, count), ALU.subtract))
                chain(nc.vector.tensor_tensor(sq, y, y, ALU.mult))
                chain(nc.vector.tensor_reduce(out=s2, in_=sq, axis=AX, op=ALU.add))
                nc.vector.tensor_scalar(s2, s2, 1.0 / H, EPS, ALU.mult, ALU.add).then_inc(var_made, 1)
                dve.wait_ge(root_made, roots[0])
                chain(nc.vector.reciprocal(inv, stats[:, 3, 0:count]))
                return wide(inv, count)

            dve.sem_inc(tile_turned, RAW)
            dve.wait_ge(consts_loaded, DMA * 6)
            chain(nc.vector.tensor_tensor(scales[:, 0:1], par[:, 0:1], par[:, 1:2], ALU.mult))
            chain(nc.vector.tensor_tensor(scales[:, 1:2], par[:, 2:3], par[:, 3:4], ALU.mult))
            chain(nc.vector.tensor_scalar(wu[:, :], wu[:, :], scales[:, 0:1], None, ALU.mult))
            chain(nc.vector.tensor_scalar(wi[:, :], wi[:, :], scales[:, 1:2], None, ALU.mult))
            dve.wait_ge(diag_turned, 1)
            chain(nc.vector.tensor_copy(diag[:, :], t_bank[:, 0:NB]))
            dve.wait_ge(x_loaded, DMA)
            for g in DOWN:
                b = slice(g * GB, (g + 1) * GB)
                nc.vector.tensor_tensor(terms[:, b, 0:H], e[:, b, :], wide(diag[:, b], GB), ALU.mult)\
                    .then_inc(x_scaled, 1)
            for n, g in enumerate(DOWN):
                b = slice(g * GB, (g + 1) * GB)
                dve.wait_ge(e_product, n + 1)
                nc.vector.tensor_tensor(e[:, b, :], by_chunk(banks[n % 2][:, 0:GB * H], H), e[:, b, :], ALU.add)\
                    .then_inc(e_made, 1)

            dve.sem_inc(at_copied[1], 1)
            with dve.Fori(0, NJ - 1) as j:
                for k in range(NS):
                    for cc in range(PB):
                        n = j * (NS * PB) + (k * PB + cc)
                        dve.wait_ge(at_made[1], n + 1)
                        dve.wait_ge(at_used[1], n + 1)
                        nc.vector.tensor_copy(at_turned[cc][1], turn_bank[1][:, :]).then_inc(at_copied[1], 1)

            dve.wait_ge(late_loaded, DMA * 5)
            lo, hi = slice(0, H), slice(H, P)
            nc.vector.tensor_tensor(w_p[:, :], w[lo, 0, :], w[lo, 2, :], ALU.subtract).then_inc(weights_made, 1)
            nc.vector.tensor_tensor(w_sums1[lo, :], w[lo, 1, :], w[lo, 3, :], ALU.subtract).then_inc(weights_made, 1)
            nc.vector.tensor_scalar(w_sums1[hi, :], w[hi, 2, :], 2.0, None, ALU.mult).then_inc(weights_made, 1)
            nc.vector.tensor_scalar(w_sums2[lo, :], w[lo, 2, :], 2.0, None, ALU.mult).then_inc(weights_made, 1)
            nc.vector.tensor_scalar(w_sums2[hi, :], w[hi, 3, :], 2.0, None, ALU.mult).then_inc(weights_made, 1)
            nc.vector.tensor_scalar(w_sums3[:, :], w[:, 3, :], 2.0, None, ALU.mult).then_inc(weights_made, 1)

            def turn_tile(t, slot, place, loads):
                dve.wait_ge(raw_loaded[slot], loads)
                dve.wait_ge(tile_used, t + 1)
                nc.vector.transpose(turned[:, place, :].rearrange("p (c b i) -> p b c i", c=GB, i=Q32),
                                    raw[:, slot, :].rearrange("p (b c i) -> p b c i", c=GB, i=Q32))\
                    .then_inc(tile_turned, 1)

            turn_tile(0, 0, 0, DMA * NQ)
            turn_tile(1, 1, 1, DMA * NQ)
            dve.wait_ge(xq_made, 1)
            for n, s in enumerate(SEGS):
                y, sq = by_chunk(scratch[:, 2 + n % 2, :], H), by_chunk(squares[:, :], H)
                k = slice(2 * s * GB, 2 * (s + 1) * GB)
                dve.wait_ge(y_copied, n + 1)
                chain(nc.vector.tensor_tensor(y, y, center(y, sq, 2 * GB), ALU.mult))
                chain(nc.vector.tensor_tensor(y, y, rows[:, 0:1, :].to_broadcast([P, 2 * GB, H]), ALU.mult))
                chain(nc.vector.tensor_tensor(y, y, xq[:, k, :], ALU.add))
                nc.vector.tensor_tensor(terms[:, k, 0:H], y, center(y, sq, 2 * GB), ALU.mult).then_inc(normed, 1)
                for t in {NS - 3: (2, 3), NS - 2: (4, 5), NS - 1: range(6, NG)}.get(n, ()):
                    turn_tile(t, t % RAW, t % TURNED, DMA * NQ * (t // RAW + 1))

            def write_q(n, chunks):
                dve.wait_ge(row_back, n + 1)
                got = by_chunk(back_bank[:, :], PH)
                nc.vector.tensor_copy(terms[:, chunks, H:2 * H], got[:, :, 0:H])
                nc.vector.scalar_tensor_tensor(out=r_start[:, chunks, :], in0=got[:, :, H:PH], scalar=2.0,
                                               in1=terms[:, chunks, 0:H], op0=ALU.mult, op1=ALU.subtract)\
                    .then_inc(row_written, 1)

            def write_r(n, g):
                dve.wait_ge(row_back, n + 1)
                k = slice(g * GB, (g + 1) * GB)
                nc.vector.scalar_tensor_tensor(out=terms[:, k, 2 * H:3 * H], in0=by_chunk(back_bank[:, 0:GB * H], H),
                                               scalar=2.0, in1=r_start[:, k, :], op0=ALU.mult, op1=ALU.add)\
                    .then_inc(row_written, 1)

            def sweep1_tiles(two, i_from, i_to):
                for i in range(i_from, i_to):
                    turn_tile(two * PAIR + i, i % RAW, i % TURNED,
                              two * (DMA * NQ * PAIR // RAW) + DMA * NQ * (i // RAW + 1))

            sweep1_tiles(0, NG, NG + 2)
            write_q(0, slice(0, GB))
            sweep1_tiles(0, NG + 2, PAIR)
            with dve.Fori(1, NG // 2) as two:
                for r in range(2):
                    row = two * 2 + (r - 1)
                    sweep1_tiles(two, r * NG, r * NG + 2)
                    write_q(row, bass.ds(row * GB, GB))
                    sweep1_tiles(two, r * NG + 2, (r + 1) * NG)

            def late_tile(n):
                turn_tile(T2 + n, (T2 + n) % RAW, (T2 + n) % TURNED, DMA * NQ * ((T2 + n) // RAW + 1))

            def finish(n, g):
                y, sq = by_chunk(scratch[:, 2 + n % 2, 0:GB * H], H), by_chunk(squares[:, 0:GB * H], H)
                k = slice(g * GB, (g + 1) * GB)
                if n >= 2:
                    dve.wait_ge(out_stored[n % 2], DMA * NQ * (n // 2))
                dve.wait_ge(out_summed, n + 1)
                nc.vector.tensor_tensor(y, by_chunk(out_bank[n % 2][:, 0:GB * H], H), terms[:, k, 0:H], ALU.add)\
                    .then_inc(out_taken, 1)
                dve.wait_ge(out_taken, n + 1)
                chain(nc.vector.tensor_tensor(y, y, rows[:, 2:3, :].to_broadcast([P, GB, H]), ALU.add))
                nc.vector.tensor_tensor(y, y, center(y, sq, GB), ALU.mult).then_inc(out_made, 1)

            n = 0
            for i, g in enumerate(DOWN):
                for k in range(NG - g):
                    late_tile(n)
                    n += 1
                    if i == 0:
                        write_q(NG - 1, slice((NG - 1) * GB, NG * GB))
                    elif k == 1:
                        write_r(ROWS1 + i - 1, DOWN[i - 1])
            for i, g in enumerate(DOWN):
                for k in range(g + 1):
                    late_tile(n)
                    n += 1
                    if i == 0 and k == 1:
                        write_r(ROWS2 - 1, DOWN[-1])
                    if i > 0 and k == min(1, g):
                        finish(i - 1, DOWN[i - 1])
            finish(NG - 1, DOWN[-1])

        @block.scalar
        def _(act):
            for n in range(NG):
                act.wait_ge(x_turned, n + 1)
                if n >= 2:
                    act.wait_ge(e_product, n - 1)
                nc.scalar.copy(scratch[0:H, n % 2, :], turn_bank[n % 2][0:H, :]).then_inc(x_copied, 1)

            act.sem_inc(at_copied[0], 1)

            def copy_turned(gg, cc, n):
                act.wait_ge(at_made[gg], n + 1)
                act.wait_ge(at_used[gg], n + 1)
                nc.scalar.copy(at_turned[cc][gg], turn_bank[gg][:, :]).then_inc(at_copied[gg], 1)

            def keep_t(slot, j):
                act.wait_ge(t_summed, j + 1)
                nc.scalar.copy(t_sum[:, :], t_bank[:, 0:PW]).then_inc(t_copied, 1)
                act.wait_ge(t_combined, j + 1)
                nc.scalar.copy(t_cols[:, slot, :], t_bank[:, PW:PW + PB * H]).then_inc(t_ready, 1)

            def layer0_panel(slot, j):
                for u in range(NS * PB):
                    copy_turned(0, u % PB, (j - 1) * (NS * PB) + u)
                keep_t(slot, j)

            keep_t(0, 0)
            with act.Fori(0, NJ // 2 - 1) as two:
                layer0_panel(1, two * 2 + 1)
                layer0_panel(0, two * 2 + 2)
            layer0_panel(1, NJ - 1)

            def take_h(n, s):
                for gg in range(2):
                    act.wait_ge(at_used[gg], PB + (NJ - 1) * (NS * PB) + (n + 1) * PB)
                nc.scalar.copy(split(scratch[:, n % 2, :]), chunk_order(h_bank[s][:, :])).then_inc(h_copied, 1)

            def take_y(n, s):
                act.wait_ge(h_turned, n + 1)
                if n >= 2:
                    act.wait_ge(normed, n - 1)
                nc.scalar.copy(scratch[:, 2 + n % 2, :].rearrange("p (g c f) -> p c g f", g=2, f=H),
                               h_bank[s][:, :].rearrange("p (c g f) -> p c g f", g=2, f=H)).then_inc(y_copied, 1)

            def root(n, count):
                act.wait_ge(var_made, n + 1)
                nc.scalar.activation(stats[:, 3, 0:count], stats[:, 1, 0:count], ACT.Sqrt).then_inc(root_made, 1)

            for k, s in enumerate(SEGS):
                for cc in range(PB):
                    for gg in range(2):
                        copy_turned(gg, cc, (NJ - 1) * (NS * PB) + k * PB + cc)
                    if k >= 1:
                        (take_h, take_y)[cc](k - 1, SEGS[k - 1])
                if k >= 2:
                    root(2 * k - 4, 2 * GB)
                    root(2 * k - 3, 2 * GB)
            take_h(NS - 1, SEGS[-1])
            take_y(NS - 1, SEGS[-1])
            for n in range(2 * NS - 4, 2 * NS):
                root(n, 2 * GB)

            def take_row(n, parity, tiles, kept):
                act.wait_ge(tile_used, TURNED + tiles)
                nc.scalar.copy(split(scratch[:, parity, :]), chunk_order(sum_bank[parity][:, :])).then_inc(row_copied, 1)
                if kept is not None:
                    act.wait_ge(row_copied, n + 1)
                    nc.scalar.copy(kept, scratch[:, parity, :]).then_inc(row_kept, 1)

            take_row(0, 0, NG, sums1[:, 0:BANK])
            take_row(1, 1, 2 * NG, sums1[:, BANK:2 * BANK])
            with act.Fori(1, NG // 2) as two:
                for r in range(2):
                    take_row(two * 2 + r, r, (two * 2 + r + 1) * NG, sums1[:, bass.ds((two * 2 + r) * BANK, BANK)])
            for i, g in enumerate(DOWN):
                take_row(ROWS1 + i, i % 2, row_end[ROWS1 + i], sums2[:, g * BANK:(g + 1) * BANK])
            for i, g in enumerate(DOWN):
                if i >= 1:
                    root(2 * NS + i - 1, GB)
                take_row(ROWS2 + i, i % 2, row_end[ROWS2 + i], None)
                act.wait_ge(pt_turned, i + 1)
                if i >= 1:
                    act.wait_ge(out_summed, i)
                nc.scalar.copy(p_turned, pt_bank[0:H, :]).then_inc(pt_copied, 1)
            root(2 * NS + NG - 1, GB)

        @block.tensor
        def _(pe):
            pe.sem_inc(seg_done, 2 * NS)
            pe.sem_inc(at_used[0], PB)
            pe.sem_inc(at_used[1], PB)
            pe.sem_inc(tile_used, TURNED)
            pe.wait_ge(ident_made, 2)
            pe.wait_ge(consts_loaded, DMA * 6)
            nc.tensor.transpose(t_bank[:, 0:NB], diag_rows[:, :], ident[0:NB, 0:NB]).then_inc(diag_turned, 1)

            def turn_x(n, g):
                pe.wait_ge(x_scaled, n + 1)
                if n >= 2:
                    pe.wait_ge(x_copied, n - 1)
                for c in range(GB):
                    last = nc.tensor.transpose(turn_bank[n % 2][0:H, c * P:(c + 1) * P],
                                               terms[:, g * GB + c, 0:H], ident[:, :])
                last.then_inc(x_turned, 1)

            def multiply_x(n, g):
                pe.wait_ge(x_copied, n + 1)
                if n >= 2:
                    pe.wait_ge(e_made, n - 1)
                for c in range(GB):
                    W = wu if g * GB + c < UB else wi
                    last = nc.tensor.matmul(banks[n % 2][:, c * H:(c + 1) * H], scratch[0:H, n % 2, c * P:(c + 1) * P],
                                            W[:, :], start=True, stop=True)
                last.then_inc(e_product, 1)

            turn_x(0, DOWN[0])
            for n, g in enumerate(DOWN):
                if n + 1 < NG:
                    turn_x(n + 1, DOWN[n + 1])
                multiply_x(n, g)
            pe.wait_ge(e_made, NG)

            def add_t(slot, k, half, half_count, signal=None):
                s = SEGS[k]
                last = None
                for b in range(half * SB // half_count, (half + 1) * SB // half_count):
                    odd = b % 2
                    if last and signal:
                        last.then_inc(signal, 1)
                        signal = None
                    last = nc.tensor.matmul(t_bank[H * odd:H * (odd + 1), 0:PW], e[:, s * SB + b, :],
                                            panels[slot][:, s * SB + b, :], start=(k == 0 and b < 2),
                                            stop=(k == NS - 1 and b >= SB - 2))
                return last

            def turn_blocks(slot, k, cc, n):
                s = SEGS[k]
                for gg in range(2):
                    pe.wait_ge(at_copied[gg], n + 1)
                    for b in range(GB):
                        last = nc.tensor.transpose(turn_bank[gg][:, b * P:(b + 1) * P],
                                                   panels[slot][:, s * SB + gg * GB + b, cc * P:(cc + 1) * P],
                                                   ident[:, :])
                    last.then_inc(at_made[gg], 1)

            def add_h(slot, k, cc, n, stop):
                for gg in range(2):
                    pe.wait_ge(at_copied[gg], n + 2)
                    last = nc.tensor.matmul(h_bank[SEGS[k]][H * gg:H * (gg + 1), :], t_cols[:, slot, cc * H:(cc + 1) * H],
                                            at_turned[cc][gg], start=False, stop=stop, skip_group_check=True)
                    last.then_inc(at_used[gg], 1)

            def combine_t(j):
                pe.wait_ge(t_copied, j + 1)
                for cc in range(PB):
                    last = nc.tensor.matmul(t_bank[:, PW + cc * H:PW + (cc + 1) * H], t_sum[:, cc * P:(cc + 1) * P],
                                            both[:, :], start=True, stop=True)
                last.then_inc(t_combined, 1)

            def layer0_panel(slot, j, loads):
                units = [(k, cc) for k in range(NS) for cc in range(PB)]
                for u, (k, cc) in enumerate(units):
                    n = (j - 1) * len(units) + u
                    turn_blocks(1 - slot, k, cc, n)
                    if u == 0:
                        pe.wait_ge(t_ready, j)
                    if cc == 0:
                        pe.wait_ge(seg_loaded[slot][SEGS[k]], loads)
                    last = add_t(slot, k, cc, PB, seg_done if cc == PB - 1 else None)
                    if u == len(units) - 1:
                        last.then_inc(t_summed, 1)
                    if u > 0:
                        add_h(1 - slot, *units[u - 1], n - 1, False)
                add_h(1 - slot, *units[-1], n, False)
                combine_t(j)

            for k in range(NS):
                pe.wait_ge(seg_loaded[0][SEGS[k]], DMA)
                last = add_t(0, k, 0, 1)
            last.then_inc(t_summed, 1)
            pe.wait_ge(zeroed, 1)
            for s in SEGS:
                nc.tensor.matmul(h_bank[s][:, :], zeros[:, 0:P], zeros[:, :], start=True, stop=False,
                                 skip_group_check=True)
            combine_t(0)
            with pe.Fori(0, NJ // 2 - 1) as two:
                layer0_panel(1, two * 2 + 1, (two + 1) * DMA)
                layer0_panel(0, two * 2 + 2, (two + 2) * DMA)
            layer0_panel(1, NJ - 1, (NJ // 2) * DMA)

            def turn_h(n, s):
                pe.wait_ge(h_copied, n + 1)
                for c in range(GB):
                    last = nc.tensor.transpose(h_bank[s][:, c * P:(c + 1) * P], scratch[:, n % 2, c * P:(c + 1) * P],
                                               ident[:, :])
                last.then_inc(h_turned, 1)

            pe.wait_ge(t_ready, NJ)
            units = [(k, cc) for k in range(NS) for cc in range(PB)]
            for u, (k, cc) in enumerate([*units, (NS, 0), (NS, 1)]):
                n = (NJ - 1) * len(units) + u
                if k < NS:
                    turn_blocks(1, k, cc, n)
                if cc == 1 and k >= 1:
                    turn_h(k - 1, SEGS[k - 1])
                if 0 < u <= len(units):
                    add_h(1, *units[u - 1], n - 1, cc == 0)

            def add_tile(t, place, c, parity, first, last_tile, columns, middle=None):
                pe.wait_ge(tile_turned, t + 1 + RAW)
                for i in range(GB):
                    if i == GB // 2 and middle:
                        middle()
                    last = nc.tensor.matmul(sum_bank[parity][:, :], terms[:, c * GB + i, columns],
                                            turned[:, place, i * BANK:(i + 1) * BANK],
                                            start=(first and i == 0), stop=(last_tile and i == GB - 1))
                last.then_inc(tile_used, 1)

            def add_tile_halves(t, place, c, parity, first, last_tile, middle=None):
                pe.wait_ge(tile_turned, t + 1 + RAW)
                for i in range(GB):
                    if i == GB // 2 and middle:
                        middle()
                    odd = i % 2
                    last = nc.tensor.matmul(sum_bank[parity][H * odd:H * (odd + 1), :],
                                            terms[:, c * GB + i, 2 * H:3 * H],
                                            turned[:, place, i * BANK:(i + 1) * BANK],
                                            start=(first and i < 2), stop=(last_tile and i >= GB - 2))
                last.then_inc(tile_used, 1)

            def turn_row(n, parity, width):
                pe.wait_ge(row_copied, n + 1)
                for c in range(GB):
                    last = nc.tensor.transpose(back_bank[:, c * width:(c + 1) * width],
                                               scratch[0:width, parity, c * P:(c + 1) * P], ident[0:width, 0:width])
                last.then_inc(row_back, 1)

            def sweep1_row(row, parity, tile, first_row=False):
                for k, c in enumerate(DOWN):
                    if first_row and k % 2 == 0:
                        pe.wait_ge(normed, k // 2 + 1)
                    if k == 1 and not first_row:
                        pe.wait_ge(row_written, row)
                    middle = (lambda: turn_row(row - 1, 1 - parity, PH)) if k == 0 and not first_row else None
                    add_tile(tile + k, (parity * NG + k) % TURNED, c, parity, k == 0, k == NG - 1,
                             slice(0, PH), middle)

            pe.wait_ge(zeroed, 2)
            sweep1_row(0, 0, 0, first_row=True)
            sweep1_row(1, 1, NG)
            with pe.Fori(1, NG // 2) as two:
                for r in range(2):
                    sweep1_row(two * 2 + r, r, two * PAIR + r * NG)

            t = T2
            for i, g in enumerate(DOWN):
                mine = [c for row, c in sweep2 if row == g]
                before = ROWS1 + i - 1
                if i == 0:
                    turn_row(before, 1, PH)
                for k, c in enumerate(mine):
                    if k == len(mine) - 1:
                        pe.wait_ge(row_written, before + 1)
                    middle = (lambda: turn_row(before, 1 - i % 2, H)) if k == 0 and i > 0 else None
                    add_tile(t, t % TURNED, c, i % 2, k == 0, k == len(mine) - 1, slice(H, 3 * H), middle)
                    t += 1

            def turn_p(i, g):
                for c in range(GB):
                    last = nc.tensor.transpose(pt_bank[0:H, c * P:(c + 1) * P], terms[:, g * GB + c, 0:H], ident[:, :])
                last.then_inc(pt_turned, 1)

            def output(i, g):
                pe.wait_ge(row_copied, ROWS2 + i + 1)
                pe.wait_ge(row_kept, ROWS2)
                pe.wait_ge(weights_made, 6)
                pe.wait_ge(pt_copied, i + 1)
                if i >= 2:
                    pe.wait_ge(out_taken, i - 1)
                for c in range(GB):
                    o = out_bank[i % 2][:, c * H:(c + 1) * H]
                    at = slice(g * BANK + c * P, g * BANK + (c + 1) * P)
                    here = slice(c * P, (c + 1) * P)
                    nc.tensor.matmul(o, sums1[:, at], w_sums1[:, :], start=True, stop=False)
                    nc.tensor.matmul(o, sums2[:, at], w_sums2[:, :], start=False, stop=False)
                    nc.tensor.matmul(o, scratch[:, i % 2, here], w_sums3[:, :], start=False, stop=False)
                    last = nc.tensor.matmul(o, p_turned[:, here], w_p[:, :], start=False, stop=True)
                last.then_inc(out_summed, 1)

            for i, g in enumerate(DOWN):
                for k in range(g + 1):
                    c = g - k
                    middle = None
                    if k == 0 and i == 0:
                        middle = lambda: turn_row(ROWS2 - 1, 1, H)
                    elif k == 0:
                        middle = lambda: turn_p(i - 1, DOWN[i - 1])
                    if i == 0 and k == g:
                        pe.wait_ge(row_written, ROWS2)
                    add_tile_halves(t, t % TURNED, c, i % 2, k == 0, k == g, middle)
                    t += 1
                    if k == 0 and i > 0:
                        output(i - 1, DOWN[i - 1])
            turn_p(NG - 1, DOWN[-1])
            output(NG - 1, DOWN[-1])


_INS = ["x", "adj", "L0_gnn_W_u", "L0_gnn_diag_u", "L0_gnn_par_u", "L0_gnn_W_i", "L0_gnn_diag_i", "L0_gnn_par_i",
        "L0_gnn_ln_gamma", "L0_gnn_ln_beta", "L1_gnn_weight", "L1_gnn_bias"]


def kernel(**inputs):
    import numpy as _np
    import concourse.bacc as _bacc
    from concourse.bass_utils import run_bass_kernel_spmd as _run

    nc = _bacc.Bacc("TRN2", target_bir_lowering=False, num_devices=1)
    arrays, args = {}, []
    for name in _INS:
        a = _np.ascontiguousarray(inputs[name])
        arrays[f"in_{name}"] = a
        args.append(nc.dram_tensor(f"in_{name}", a.shape, mybir.dt.from_np(a.dtype), kind="ExternalInput").ap())
    shape = inputs["x"].shape
    args.append(nc.dram_tensor("out_0", shape, F32, kind="ExternalOutput").ap())
    resnorm_chebyshev(nc, *args)
    r = _run(nc, [arrays], core_ids=[0])
    return r.results[0]["out_0"]
```

```python
from contextlib import ExitStack

import concourse.bass as bass
from concourse import mybir

F32 = mybir.dt.float32
BF16 = mybir.dt.bfloat16
ALU = mybir.AluOpType
ACT = mybir.ActivationFunctionType
AX = mybir.AxisListType.X

P = 128
H = 64
PH = 2 * H
Q32 = 32
BANK = 512
PW = 256
PB = PW // P
NQ = P // Q32
EPS = 1e-5
RAW = 4
TURNED = 2
MORE_RAW = 3
MORE_TURNED = 2
AT = 4
DMA = 16


def resnorm_chebyshev(nc, x, adj, W_u, diag_u, par_u, W_i, diag_i, par_i, gamma, beta, weight, bias, out):
    N = adj.shape[0]
    NU = diag_u.shape[0]
    NB = N // P
    NG = N // BANK
    NJ = N // PW
    GB = BANK // P
    NS = NG // 2
    SB = 2 * GB
    UB = NU // P
    assert x.shape[1] == H and N % (2 * BANK) == 0 and NU % P == 0 and NG % 2 == 0 and NJ % 2 == 0
    assert (2 * NG) % RAW == 0 and (2 * NG) % TURNED == 0 and UB % 2 == 0

    with ExitStack() as ctx:
        def sb(name, shape, dt=F32):
            return ctx.enter_context(nc.sbuf_tensor(name, shape, dt))

        def sem(name):
            return ctx.enter_context(nc.semaphore(name))

        panel_size = NB * PW
        shared = sb("shared", [P, 2 * panel_size + NB * H + AT * BANK])
        panels = [shared[:, k * panel_size:(k + 1) * panel_size].rearrange("p (b c) -> p b c", c=PW)
                  for k in range(2)]
        at = 2 * panel_size
        e = shared[:, at:at + NB * H].rearrange("p (b f) -> p b f", f=H)
        at += NB * H
        at_turned = [shared[:, at + k * BANK:at + (k + 1) * BANK] for k in range(AT)]
        sums1 = shared[:, 0:N]
        sums2 = shared[:, N:2 * N]
        norm_squares = [shared[:, N + n * BANK:N + (n + 1) * BANK] for n in range(NS)]
        norm_terms = [shared[:, N + (NS + n) * BANK:N + (NS + n + 1) * BANK] for n in range(NS)]
        at = 2 * N
        r_start = shared[:, at:at + NB * H].rearrange("p (k f) -> p k f", f=H)
        at += NB * H
        p_turned = shared[0:H, at:at + BANK]
        at += BANK
        o_turned = shared[:, at:at + BANK]
        at += BANK

        terms = sb("terms", [P, NB, 3 * H])
        xq = sb("xq", [P, NB, H])
        tile_size = GB * BANK
        raw_base = sb("raw", [P, RAW * tile_size])
        turned_base = sb("turned", [P, TURNED * tile_size])
        raw = [raw_base[:, k * tile_size:(k + 1) * tile_size] for k in range(RAW)]
        turned = [turned_base[:, k * tile_size:(k + 1) * tile_size] for k in range(TURNED)]
        more = [shared[:, at + k * tile_size:at + (k + 1) * tile_size] for k in range(MORE_RAW + MORE_TURNED)]
        raw += more[:MORE_RAW]
        turned += more[MORE_RAW:]
        ident = sb("ident", [P, P])
        centre = sb("centre", [P, P])
        centre_gamma = sb("centre_gamma", [P, P])
        both = sb("both", [P, H])
        zeros = sb("zeros", [P, BANK], BF16)
        t_sum = sb("t_sum", [P, PW])
        t_cols = sb("t_cols", [P, 2, PB * H])
        t_quart = sb("t_quart", [P, GB * H])
        scratch = sb("scratch", [P, 4, BANK])
        squares = sb("squares", [P, BANK])
        stats = sb("stats", [P, 3, 2 * GB])
        w_pair = sb("w_pair", [P, 2, PH])
        par = sb("par", [P, 4])
        scales = sb("scales", [P, 2])
        diag_rows = sb("diag_rows", [NB, P])
        diag = sb("diag", [P, NB])
        w = sb("w", [P, 4, H])
        w_sums1 = sb("w_sums1", [P, H])
        w_sums2 = sb("w_sums2", [P, H])
        w_sums3 = sb("w_sums3", [P, H])
        w_p = sb("w_p", [H, H])
        rows = sb("rows", [P, 3, H])
        bias_column = sb("bias_column", [P, 1])

        banks = [ctx.enter_context(nc.psum_tensor(f"bank{i}", [P, BANK], F32)) for i in range(8)]
        h_bank = banks[0:NS]
        t_bank = banks[5]
        turn_bank = banks[6:8]
        sum_bank = banks[6:8]
        back_bank = banks[5]
        pt_bank = banks[4]
        o_bank = banks[3]
        out_bank = banks[1:3]

        consts_loaded = sem("consts_loaded")
        x_loaded = sem("x_loaded")
        xq_loaded = sem("xq_loaded")
        xq_made = sem("xq_made")
        late_loaded = sem("late_loaded")
        zeroed = sem("zeroed")
        ident_made = sem("ident_made")
        diag_turned = sem("diag_turned")
        x_scaled = sem("x_scaled")
        x_turned = sem("x_turned")
        x_copied = sem("x_copied")
        e_product = sem("e_product")
        e_made = sem("e_made")
        seg_loaded = [[sem(f"seg_loaded{k}_{s}") for s in range(NS)] for k in range(2)]
        seg_done = sem("seg_done")
        at_made = sem("at_made")
        at_copied = sem("at_copied")
        at_used = sem("at_used")
        t_summed = sem("t_summed")
        t_copied = sem("t_copied")
        t_combined = sem("t_combined")
        t_ready = sem("t_ready")
        t_quartered = sem("t_quartered")
        h_copied = sem("h_copied")
        h_turned = sem("h_turned")
        y_copied = sem("y_copied")
        normed = sem("normed")
        dve_step = sem("dve_step")
        pool_step = sem("pool_step")
        var_made = sem("var_made")
        root_made = sem("root_made")
        w_cleared = sem("w_cleared")
        raw_loaded = [sem(f"raw_loaded{k}") for k in range(RAW + MORE_RAW)]
        tile_turned = sem("tile_turned")
        tile_used = sem("tile_used")
        row_copied = sem("row_copied")
        row_kept = sem("row_kept")
        row_back = sem("row_back")
        row_written = sem("row_written")
        weights_made = sem("weights_made")
        xq_step = sem("xq_step")
        pt_turned = sem("pt_turned")
        pt_copied = sem("pt_copied")
        o_summed = sem("o_summed")
        o_copied = sem("o_copied")
        out_summed = sem("out_summed")
        out_taken = sem("out_taken")
        out_made = sem("out_made")
        out_stored = [sem(f"out_stored{k}") for k in range(2)]

        SEGS = [NS - 1 - k for k in range(NS)]
        DOWN = [NG - 1 - k for k in range(NG)]

        TILED = NS - 1
        ITEMS = [(k, cc, gg) for k in range(NS) for cc in range(PB) for gg in range(1 if k < TILED else 2)]
        T1 = TILED * NG
        assert TILED == RAW and T1 % RAW == 0 and TILED // 2 * GB <= NS * PB and len(ITEMS) % AT == 0

        sweep2 = [(g, c) for g in DOWN for c in [*range(NG - 1, g + 1, -1), g, *([g + 1] if g + 1 < NG else [])]]
        sweep3 = [(g, c) for g in DOWN for c in range(g, -1, -1)]
        T2 = T1 + NG * NG
        late_tiles = sweep2 + sweep3
        row_end = {n: T1 + (n + 1) * NG for n in range(NG)}
        for n in range(NG, 3 * NG):
            row_end[n] = row_end[n - 1] + (n - NG + 1 if n < 2 * NG else 3 * NG - n)
        PAIR = 2 * NG

        def late_slots(n):
            found = []
            for base, count in ((RAW, RAW + MORE_RAW), (TURNED, TURNED + MORE_TURNED)):
                slot = n % count
                before = T2 // base if slot < base else 0
                last = T2 + n - count if n >= count else (T2 - base + slot if slot < base else None)
                found += [slot, before + n // count, last]
            return found

        ROWS1, ROWS2 = NG, 2 * NG

        def by_chunk(a, width):
            return a.rearrange("p (k f) -> p k f", f=width)

        def wide(a, count):
            return a.rearrange("p (k o) -> p k o", o=1).to_broadcast([P, count, H])

        def quarter(a, g, q):
            return a[BANK * g + P * q:BANK * g + P * (q + 1), :].rearrange("(c j) f -> j c f", j=Q32)

        def chunk_order(a):
            return a.rearrange("p (q c j) -> p c q j", q=NQ, j=Q32)

        def split(a):
            return a.rearrange("p (c q j) -> p c q j", q=NQ, j=Q32)

        block = ctx.enter_context(nc.Block())

        @block.sync
        def _(sp):
            sp.dma_start(diag_rows[0:UB, :], diag_u.rearrange("(b p) -> b p", p=P)).then_inc(consts_loaded, DMA)
            sp.dma_start(diag_rows[UB:NB, :], diag_i.rearrange("(b p) -> b p", p=P)).then_inc(consts_loaded, DMA)
            sp.dma_start(e[:, :, :], x.rearrange("(b p) f -> p b f", p=P)).then_inc(x_loaded, DMA)
            sp.wait_ge(w_cleared, 1)
            for k, a in enumerate((W_u, W_i)):
                for half in range(2):
                    rows_of = slice(H * half, H * (half + 1))
                    sp.dma_start(w_pair[rows_of, k, rows_of], a).then_inc(consts_loaded, DMA)
            for k, a in enumerate((par_u, par_i)):
                sp.dma_start(par[:, 2 * k:2 * k + 2], a.rearrange("(o n) -> o n", o=1).to_broadcast([P, 2]))\
                    .then_inc(consts_loaded, DMA)

            seg_rows = adj.rearrange("(s b p) c -> s p b c", p=P, b=SB)
            block_rows = adj.rearrange("(b i) c -> i b c", i=Q32)
            tile_rows = adj.rearrange("(g b i) c -> g i b c", b=BANK // Q32, i=Q32)

            def load_tile(slot, last, first_block, column):
                if last is not None:
                    sp.wait_ge(tile_turned, last + 1 + RAW)
                for q in reversed(range(NQ)):
                    sp.dma_start(raw[slot][Q32 * q:Q32 * (q + 1), :].rearrange("p (b c) -> p b c", c=P),
                                 block_rows[:, bass.ds(first_block, BANK // Q32), column + P * q:column + P * (q + 1)])\
                        .then_inc(raw_loaded[slot], DMA)

            def load_layer0_tile(k, last, column):
                if last is not None:
                    sp.wait_ge(tile_turned, last + 1 + RAW)
                for q in range(NQ):
                    sp.dma_start(raw[k][Q32 * q:Q32 * (q + 1), :].rearrange("p (b c) -> p b c", c=P),
                                 tile_rows[2 * SEGS[k] + 1][:, :, bass.ds(column + P * q, P)])\
                        .then_inc(raw_loaded[k], DMA)

            def load_panel(slot, uses, column, tiles=()):
                for k, s in enumerate(SEGS):
                    sp.wait_ge(seg_done, (uses * 2 + slot) * NS + (k + 1))
                    sp.dma_start(panels[slot][:, s * SB:(s + 1) * SB, :], seg_rows[s][:, :, bass.ds(column, PW)])\
                        .then_inc(seg_loaded[slot][s], DMA)
                    if tiles and k in (1, 3):
                        load_layer0_tile(*tiles[k // 2])

            load_panel(0, 0, 0)
            load_panel(1, 0, PW, [(0, None, 0), (1, None, 0)])
            with sp.Fori(2, NJ // 2 + 1) as pair:
                end = sp.snap(pair * BANK)
                for slot in range(2):
                    load_panel(slot, pair - 1, end + (slot - 2) * PW,
                               [((2 * slot + 2 + n) % RAW, (pair - 1) * TILED + (2 * slot - 2 + n - RAW),
                                 end + (slot - 2) * BANK) for n in range(2)])
            for n in range(2, TILED):
                load_layer0_tile(n, T1 - TILED + n - RAW, (NG - 1) * BANK)

            with sp.Fori(0, NG // 2) as two:
                for n in range(PAIR):
                    load_tile(n % RAW, two * PAIR + (T1 + n - RAW), (two * 2 + n // NG) * (BANK // Q32), DOWN[n % NG] * BANK)
            for n, (g, c) in enumerate(late_tiles):
                slot, _, last = late_slots(n)[0:3]
                load_tile(slot, last, g * (BANK // Q32), c * BANK)

        @block.gpsimd
        def _(pool):
            nc.gpsimd.memset(ident[:, :], 0.0).then_inc(pool_step, 1)
            nc.gpsimd.memset(both[:, :], 0.0).then_inc(pool_step, 1)
            pool.wait_ge(pool_step, 2)
            nc.gpsimd.affine_select(out=ident[:, :], in_=ident[:, :], compare_op=ALU.not_equal, fill=1.0,
                                    base=0, pattern=[[-1, P]], channel_multiplier=1).then_inc(ident_made, 1)
            nc.gpsimd.affine_select(out=both[:, :], in_=both[:, :], compare_op=ALU.not_equal, fill=1.0,
                                    base=0, pattern=[[-1, H]], channel_multiplier=1).then_inc(pool_step, 1)
            pool.wait_ge(pool_step, 3)
            nc.gpsimd.affine_select(out=both[:, :], in_=both[:, :], compare_op=ALU.not_equal, fill=1.0,
                                    base=-H, pattern=[[-1, H]], channel_multiplier=1).then_inc(ident_made, 1)
            nc.gpsimd.memset(zeros[:, :], 0.0).then_inc(zeroed, 1)
            pool.wait_ge(t_ready, 1)
            for k, a in enumerate((gamma, beta, bias)):
                pool.dma_start(rows[:, k, :], a.rearrange("(o f) -> o f", o=1).to_broadcast([P, H]))\
                    .then_inc(late_loaded, DMA)
            for k in range(2):
                pool.dma_start(w[H * k:H * (k + 1), :, :], weight.rearrange("k i o -> i k o"))\
                    .then_inc(late_loaded, DMA)
            for g in range(NG):
                for q in range(NQ):
                    pool.dma_start(xq[Q32 * q:Q32 * (q + 1), g * GB:(g + 1) * GB, :], quarter(x, g, q))\
                        .then_inc(xq_loaded, DMA)
            nc.gpsimd.memset(terms[:, :, H:3 * H], 0.0).then_inc(zeroed, 1)
            pool.wait_ge(late_loaded, DMA * 5)
            pool.wait_ge(xq_loaded, DMA * NG * NQ)
            nc.gpsimd.tensor_tensor(out=xq[:, :, :], in0=xq[:, :, :], in1=xq[:, :, :], op=ALU.add)\
                .then_inc(pool_step, 1)
            pool.wait_ge(pool_step, 4)
            nc.gpsimd.tensor_tensor(out=xq[:, :, :], in0=xq[:, :, :],
                                    in1=rows[:, 1:2, :].to_broadcast([P, NB, H]), op=ALU.add).then_inc(xq_made, 1)
            for n, g in enumerate(DOWN):
                pool.wait_ge(out_made, n + 1)
                for q in range(NQ):
                    pool.dma_start(quarter(out, g, q), by_chunk(scratch[Q32 * q:Q32 * (q + 1), 2 + n % 2, 0:GB * H], H))\
                        .then_inc(out_stored[n % 2], DMA)
            for k in range(2):
                pool.wait_ge(out_stored[k], DMA * NQ * (NG // 2))

        @block.vector
        def _(dve):
            steps = [0]

            def chain(instruction):
                steps[0] += 1
                instruction.then_inc(dve_step, 1)
                dve.wait_ge(dve_step, steps[0])

            roots = [0]

            def remove_mean(a, count):
                mean = stats[:, 0, 0:count]
                chain(nc.vector.tensor_reduce(out=mean, in_=a, axis=AX, op=ALU.add))
                chain(nc.vector.tensor_scalar(mean, mean, 1.0 / H, None, ALU.mult))
                chain(nc.vector.tensor_tensor(a, a, wide(mean, count), ALU.subtract))

            def inverse_deviation(squares_of, count):
                var, inv = stats[:, 0, 0:count], stats[:, 2, 0:count]
                roots[0] += 1
                chain(nc.vector.tensor_reduce(out=var, in_=squares_of, axis=AX, op=ALU.add))
                nc.vector.tensor_scalar(var, var, 1.0 / H, EPS, ALU.mult, ALU.add).then_inc(var_made, 1)
                dve.wait_ge(root_made, roots[0])
                chain(nc.vector.reciprocal(inv, stats[:, 1, 0:count]))
                return wide(inv, count)

            dve.sem_inc(tile_turned, RAW)
            nc.vector.memset(w_pair[:, :, :], 0.0).then_inc(w_cleared, 1)
            dve.wait_ge(consts_loaded, DMA * 8)
            chain(nc.vector.tensor_tensor(scales[:, 0:1], par[:, 0:1], par[:, 1:2], ALU.mult))
            chain(nc.vector.tensor_tensor(scales[:, 1:2], par[:, 2:3], par[:, 3:4], ALU.mult))
            for k in range(2):
                chain(nc.vector.tensor_scalar(w_pair[:, k, :], w_pair[:, k, :], scales[:, k:k + 1], None, ALU.mult))
            dve.wait_ge(diag_turned, 1)
            chain(nc.vector.tensor_copy(diag[:, :], t_bank[:, 0:NB]))
            dve.wait_ge(x_loaded, DMA)
            for s in SEGS:
                b = slice(s * SB, (s + 1) * SB)
                nc.vector.tensor_tensor(xq[:, b, :], e[:, b, :], wide(diag[:, b], SB), ALU.mult).then_inc(x_scaled, 1)
            for n, s in enumerate(SEGS):
                b = slice(s * SB, (s + 1) * SB)
                dve.wait_ge(e_product, n + 1)
                nc.vector.tensor_tensor(e[:, b, :], by_chunk(banks[n % 2][:, :], H), e[:, b, :], ALU.add)\
                    .then_inc(e_made, 1)

            def turn_tile(slot, loads, place, last):
                dve.wait_ge(raw_loaded[slot], loads)
                if last is not None:
                    dve.wait_ge(tile_used, last + 1 + TURNED)
                nc.vector.transpose(turned[place].rearrange("p (c b i) -> p b c i", c=GB, i=Q32),
                                    raw[slot].rearrange("p (b c i) -> p b c i", c=GB, i=Q32))\
                    .then_inc(tile_turned, 1)

            dve.wait_ge(late_loaded, DMA * 5)
            dve.wait_ge(ident_made, 2)
            chain(nc.vector.tensor_copy(centre[:, :], ident[:, :]))
            remove_mean(by_chunk(centre[:, :], H), 2)
            chain(nc.vector.tensor_tensor(by_chunk(centre_gamma[:, :], H), by_chunk(centre[:, :], H),
                                          rows[:, 0:1, :].to_broadcast([P, 2, H]), ALU.mult))
            remove_mean(by_chunk(centre_gamma[:, :], H), 2)
            chain(nc.vector.tensor_tensor(w[:, 0, :], w[:, 0, :], both[:, :], ALU.add))
            remove_mean(w[:, :, :], 4)
            remove_mean(rows[:, 2:3, :], 1)
            chain(nc.vector.memset(bias_column[:, :], 0.0))
            chain(nc.vector.tensor_tensor(squares[0:H, 0:H], rows[0:H, 2, :], both[0:H, :], ALU.mult))
            chain(nc.vector.tensor_reduce(out=bias_column[0:H, :], in_=squares[0:H, 0:H], axis=AX, op=ALU.add))
            lo, hi = slice(0, H), slice(H, P)
            nc.vector.tensor_tensor(w_p[:, :], w[lo, 0, :], w[lo, 2, :], ALU.subtract).then_inc(weights_made, 1)
            nc.vector.tensor_tensor(w_sums1[lo, :], w[lo, 1, :], w[lo, 3, :], ALU.subtract).then_inc(weights_made, 1)
            nc.vector.tensor_scalar(w_sums1[hi, :], w[hi, 2, :], 2.0, None, ALU.mult).then_inc(weights_made, 1)
            nc.vector.tensor_scalar(w_sums2[lo, :], w[lo, 2, :], 2.0, None, ALU.mult).then_inc(weights_made, 1)
            nc.vector.tensor_scalar(w_sums2[hi, :], w[hi, 3, :], 2.0, None, ALU.mult).then_inc(weights_made, 1)
            nc.vector.tensor_scalar(w_sums3[:, :], w[:, 3, :], 2.0, None, ALU.mult).then_inc(weights_made, 1)

            def quarter_t(m):
                dve.wait_ge(t_ready, m * 2 + 2)
                for q in range(NQ):
                    for c in range(GB):
                        last = nc.vector.tensor_copy(t_quart[Q32 * q:Q32 * (q + 1), c * H:(c + 1) * H],
                                                     t_cols[Q32 * c:Q32 * (c + 1), q // PB, q % PB * H:(q % PB + 1) * H])
                last.then_inc(t_quartered, 1)

            def center_xq(g):
                part = xq[:, bass.ds(g * GB, GB), :]
                mean = stats[:, 0, 0:GB]
                dve.wait_ge(xq_made, 1)
                nc.vector.tensor_reduce(out=mean, in_=part, axis=AX, op=ALU.add).then_inc(xq_step, 1)
                dve.wait_ge(xq_step, g * 3 + 1)
                nc.vector.tensor_scalar(mean, mean, 1.0 / H, None, ALU.mult).then_inc(xq_step, 1)
                dve.wait_ge(xq_step, g * 3 + 2)
                nc.vector.tensor_tensor(part, part, wide(mean, GB), ALU.subtract).then_inc(xq_step, 1)
                dve.wait_ge(xq_step, g * 3 + 3)

            for t in range(2):
                turn_tile(t, DMA * NQ, t, t - TURNED)
            quarter_t(0)
            with dve.Fori(0, NG - 1) as m:
                for n in range(2, 2 + TILED):
                    turn_tile(n % RAW, m * (DMA * NQ) + DMA * NQ * (n // RAW + 1), n % TURNED, m * TILED + (n - TURNED))
                quarter_t(m + 1)
                center_xq(m)
            center_xq(NG - 1)
            for t in range(T1 - 2, T1):
                turn_tile(t % RAW, DMA * NQ * (t // RAW + 1), t % TURNED, t - TURNED)

            for n, s in enumerate(SEGS):
                y, sq = by_chunk(norm_terms[n], H), by_chunk(squares[:, :], H)
                k = slice(2 * s * GB, 2 * (s + 1) * GB)
                dve.wait_ge(y_copied, n + 1)
                chain(nc.vector.tensor_tensor(y, y, inverse_deviation(by_chunk(norm_squares[n], H), 2 * GB), ALU.mult))
                chain(nc.vector.tensor_tensor(y, y, xq[:, k, :], ALU.add))
                chain(nc.vector.tensor_tensor(sq, y, y, ALU.mult))
                nc.vector.tensor_tensor(terms[:, k, 0:H], y, inverse_deviation(sq, 2 * GB), ALU.mult).then_inc(normed, 1)
                for t in [T1 + i for i in ((0,), (1,), (2, 3), (4, 5), range(6, NG))[n]]:
                    turn_tile(t % RAW, DMA * NQ * (t // RAW + 1), t % TURNED, t - TURNED)

            def write_q(n, chunks):
                dve.wait_ge(row_back, n + 1)
                got = by_chunk(back_bank[:, :], PH)
                nc.vector.tensor_copy(terms[:, chunks, H:2 * H], got[:, :, 0:H])
                nc.vector.scalar_tensor_tensor(out=r_start[:, chunks, :], in0=got[:, :, H:PH], scalar=2.0,
                                               in1=terms[:, chunks, 0:H], op0=ALU.mult, op1=ALU.subtract)\
                    .then_inc(row_written, 1)

            def write_r(n, g):
                dve.wait_ge(row_back, n + 1)
                k = slice(g * GB, (g + 1) * GB)
                nc.vector.scalar_tensor_tensor(out=terms[:, k, 2 * H:3 * H], in0=by_chunk(back_bank[:, 0:GB * H], H),
                                               scalar=2.0, in1=r_start[:, k, :], op0=ALU.mult, op1=ALU.add)\
                    .then_inc(row_written, 1)

            def sweep1_tiles(two, i_from, i_to):
                for i in range(i_from, i_to):
                    turn_tile(i % RAW, two * (DMA * NQ * PAIR // RAW) + DMA * NQ * ((T1 + i) // RAW + 1),
                              i % TURNED, two * PAIR + (T1 + i - TURNED))

            sweep1_tiles(0, NG, NG + 2)
            write_q(0, slice(0, GB))
            sweep1_tiles(0, NG + 2, PAIR)
            with dve.Fori(1, NG // 2) as two:
                for r in range(2):
                    row = two * 2 + (r - 1)
                    sweep1_tiles(two, r * NG, r * NG + 2)
                    write_q(row, bass.ds(row * GB, GB))
                    sweep1_tiles(two, r * NG + 2, (r + 1) * NG)

            def late_tile(n):
                slot, uses, _, place, _, last = late_slots(n)
                turn_tile(slot, DMA * NQ * (uses + 1), place, last)

            def finish(n, g):
                y, sq = by_chunk(scratch[:, 2 + n % 2, 0:GB * H], H), by_chunk(squares[:, 0:GB * H], H)
                if n >= 2:
                    dve.wait_ge(out_stored[n % 2], DMA * NQ * (n // 2))
                dve.wait_ge(out_summed, n + 1)
                halves = by_chunk(out_bank[n % 2][:, :], PH)
                chain(nc.vector.tensor_copy(y, halves[:, :, 0:H]))
                nc.vector.tensor_tensor(y, halves[:, :, H:PH], y, ALU.add).then_inc(out_taken, 1)
                dve.wait_ge(out_taken, n + 1)
                chain(nc.vector.tensor_tensor(sq, y, y, ALU.mult))
                nc.vector.tensor_tensor(y, y, inverse_deviation(sq, GB), ALU.mult).then_inc(out_made, 1)

            n = 0
            for i, g in enumerate(DOWN):
                for k in range(NG - g):
                    late_tile(n)
                    n += 1
                    if i == 0:
                        write_q(NG - 1, slice((NG - 1) * GB, NG * GB))
                    elif k == 1:
                        write_r(ROWS1 + i - 1, DOWN[i - 1])
            for i, g in enumerate(DOWN):
                for k in range(g + 1):
                    late_tile(n)
                    n += 1
                    if i == 0 and k == 1:
                        write_r(ROWS2 - 1, DOWN[-1])
                    if i > 0 and k == min(3, g):
                        finish(i - 1, DOWN[i - 1])
            finish(NG - 1, DOWN[-1])

        @block.scalar
        def _(act):
            for n in range(NS):
                act.wait_ge(x_turned, n + 1)
                if n >= 2:
                    act.wait_ge(e_product, n - 1)
                nc.scalar.copy(scratch[:, n % 2, :], turn_bank[n % 2][:, :]).then_inc(x_copied, 1)

            act.sem_inc(at_copied, 2)

            def copy_turned(i, before):
                act.wait_ge(at_made, before + (i + 1))
                act.wait_ge(at_used, before + (i + 1))
                nc.scalar.copy(at_turned[i % AT], turn_bank[i % 2][:, :]).then_inc(at_copied, 1)

            def keep_t(slot, j):
                act.wait_ge(t_summed, j + 1)
                nc.scalar.copy(t_sum[:, :], t_bank[:, 0:PW]).then_inc(t_copied, 1)
                act.wait_ge(t_combined, j + 1)
                nc.scalar.copy(t_cols[:, slot, :], t_bank[:, PW:PW + PB * H]).then_inc(t_ready, 1)

            def layer0_panel(slot, j):
                for i in range(len(ITEMS)):
                    copy_turned(i, (j - 1) * len(ITEMS))
                keep_t(slot, j)

            keep_t(0, 0)
            layer0_panel(1, 1)
            with act.Fori(1, NJ // 2) as two:
                layer0_panel(0, two * 2)
                layer0_panel(1, two * 2 + 1)

            def take_h(n, s):
                act.wait_ge(at_used, AT + (NJ - 1) * len(ITEMS) + sum(k <= n for k, cc, gg in ITEMS))
                if n < TILED:
                    act.wait_ge(tile_used, TURNED + T1 - TILED + n + 1)
                nc.scalar.copy(split(scratch[:, n % 2, :]), chunk_order(h_bank[s][:, :])).then_inc(h_copied, 1)

            def take_y(n, s):
                act.wait_ge(h_turned, n + 1)
                nc.scalar.activation(norm_squares[n].rearrange("p (g c f) -> p c g f", g=2, f=H),
                                     h_bank[s][:, :].rearrange("p (c g f) -> p c g f", g=2, f=H), ACT.Square)
                nc.scalar.copy(norm_terms[n].rearrange("p (g c f) -> p c g f", g=2, f=H),
                               t_bank[:, :].rearrange("p (c g f) -> p c g f", g=2, f=H)).then_inc(y_copied, 1)

            def root(n, count):
                act.wait_ge(var_made, n + 1)
                nc.scalar.activation(stats[:, 1, 0:count], stats[:, 0, 0:count], ACT.Sqrt).then_inc(root_made, 1)

            for k, s in enumerate(SEGS):
                for cc in range(PB):
                    for i, item in enumerate(ITEMS):
                        if item[0:2] == (k, cc):
                            copy_turned(i, (NJ - 1) * len(ITEMS))
                    if k >= 1:
                        (take_h, take_y)[cc](k - 1, SEGS[k - 1])
                    if (k, cc) == (NS - 1, PB - 1):
                        take_h(k, SEGS[k])
                    if k >= 2:
                        root(2 * k - 4 + cc, 2 * GB)
            take_y(NS - 1, SEGS[-1])
            for n in range(2 * NS - 4, 2 * NS):
                root(n, 2 * GB)

            def take_row(n, parity, tiles, kept):
                act.wait_ge(tile_used, TURNED + tiles)
                nc.scalar.copy(split(scratch[:, parity, :]), chunk_order(sum_bank[parity][:, :])).then_inc(row_copied, 1)
                if kept is not None:
                    act.wait_ge(row_copied, n + 1)
                    nc.scalar.copy(kept, scratch[:, parity, :]).then_inc(row_kept, 1)

            take_row(0, 0, row_end[0], sums1[:, 0:BANK])
            take_row(1, 1, row_end[1], sums1[:, BANK:2 * BANK])
            with act.Fori(1, NG // 2) as two:
                for r in range(2):
                    take_row(two * 2 + r, r, (two * 2 + r + 1) * NG + T1, sums1[:, bass.ds((two * 2 + r) * BANK, BANK)])
            for i, g in enumerate(DOWN):
                take_row(ROWS1 + i, i % 2, row_end[ROWS1 + i], sums2[:, g * BANK:(g + 1) * BANK])
            def take_output(i):
                act.wait_ge(pt_turned, i + 1)
                nc.scalar.copy(p_turned, pt_bank[0:H, :]).then_inc(pt_copied, 1)
                act.wait_ge(o_summed, i + 1)
                nc.scalar.activation(o_turned, o_bank[:, :], ACT.Identity, bias=bias_column[:, :]).then_inc(o_copied, 1)

            for i, g in enumerate(DOWN):
                if i >= 1:
                    take_output(i - 1)
                    if g > 0:
                        root(2 * NS + i - 1, GB)
                take_row(ROWS2 + i, i % 2, row_end[ROWS2 + i], None)
            root(2 * NS + NG - 2, GB)
            take_output(NG - 1)
            root(2 * NS + NG - 1, GB)

        @block.tensor
        def _(pe):
            pe.sem_inc(seg_done, 2 * NS)
            pe.sem_inc(at_used, AT)
            pe.sem_inc(tile_used, TURNED)
            pe.wait_ge(ident_made, 2)
            pe.wait_ge(consts_loaded, DMA * 8)
            nc.tensor.transpose(t_bank[:, 0:NB], diag_rows[:, :], ident[0:NB, 0:NB]).then_inc(diag_turned, 1)

            def turn_x(n, s):
                pe.wait_ge(x_scaled, n + 1)
                if n >= 2:
                    pe.wait_ge(x_copied, n - 1)
                for c in range(SB // 2):
                    b = s * SB + 2 * c
                    last = nc.tensor.transpose(turn_bank[n % 2][:, c * P:(c + 1) * P],
                                               xq[:, b:b + 2, :].rearrange("p k f -> p (k f)"), ident[:, :])
                last.then_inc(x_turned, 1)

            def multiply_x(n, s):
                pe.wait_ge(x_copied, n + 1)
                if n >= 2:
                    pe.wait_ge(e_made, n - 1)
                for c in range(SB // 2):
                    items = int(s * SB + 2 * c >= UB)
                    last = nc.tensor.matmul(banks[n % 2][:, c * PH:(c + 1) * PH], scratch[:, n % 2, c * P:(c + 1) * P],
                                            w_pair[:, items, :], start=True, stop=True)
                last.then_inc(e_product, 1)

            turn_x(0, SEGS[0])
            for n, s in enumerate(SEGS):
                if n + 1 < NS:
                    turn_x(n + 1, SEGS[n + 1])
                multiply_x(n, s)

            def add_t(slot, k, half, half_count, signal=None):
                s = SEGS[k]
                last = None
                for b in range(half * SB // half_count, (half + 1) * SB // half_count):
                    odd = b % 2
                    if last and signal:
                        last.then_inc(signal, 1)
                        signal = None
                    last = nc.tensor.matmul(t_bank[H * odd:H * (odd + 1), 0:PW], e[:, s * SB + b, :],
                                            panels[slot][:, s * SB + b, :], start=(k == 0 and b < 2),
                                            stop=(k == NS - 1 and b >= SB - 2))
                return last

            UNITS = [(k, cc) for k in range(NS) for cc in range(PB)]

            def items(unit):
                return [(i, gg) for i, (k, cc, gg) in enumerate(ITEMS) if (k, cc) == unit]

            def turn_blocks(slot, unit, before):
                k, cc = unit
                for i, gg in items(unit):
                    pe.wait_ge(at_copied, before + (i + 1))
                    for b in range(GB):
                        last = nc.tensor.transpose(turn_bank[i % 2][:, b * P:(b + 1) * P],
                                                   panels[slot][:, SEGS[k] * SB + gg * GB + b, cc * P:(cc + 1) * P],
                                                   ident[:, :])
                    last.then_inc(at_made, 1)

            def add_h(slot, unit, before, stop):
                k, cc = unit
                for i, gg in items(unit):
                    pe.wait_ge(at_copied, before + (i + 3))
                    nc.tensor.matmul(h_bank[SEGS[k]][H * gg:H * (gg + 1), :], t_cols[:, slot, cc * H:(cc + 1) * H],
                                     at_turned[i % AT], start=False, stop=stop, skip_group_check=True)\
                        .then_inc(at_used, 1)

            def add_h_tile(k, c, t, stop):
                if c == 0:
                    pe.wait_ge(tile_turned, t + (1 + RAW))
                last = nc.tensor.matmul(h_bank[SEGS[k]][H:P, :], t_quart[:, c * H:(c + 1) * H],
                                        turned[k % TURNED][:, c * BANK:(c + 1) * BANK],
                                        start=False, stop=stop, skip_group_check=True)
                if c == GB - 1:
                    last.then_inc(tile_used, 1)

            def combine_t(j):
                pe.wait_ge(t_copied, j + 1)
                for cc in range(PB):
                    last = nc.tensor.matmul(t_bank[:, PW + cc * H:PW + (cc + 1) * H], t_sum[:, cc * P:(cc + 1) * P],
                                            both[:, :], start=True, stop=True)
                last.then_inc(t_combined, 1)

            def layer0_panel(slot, j, loads, group=None):
                before = (j - 1) * len(ITEMS)

                def add(u):
                    add_h(1 - slot, UNITS[u], before, False)
                    if group is not None and u < TILED // 2 * GB:
                        k = slot * (TILED // 2) + u // GB
                        if slot == 0 and u == 0:
                            pe.wait_ge(t_quartered, group + 1)
                        add_h_tile(k, u % GB, group * TILED + k, False)

                for u, (k, cc) in enumerate(UNITS):
                    turn_blocks(1 - slot, (k, cc), before)
                    if u == 0:
                        pe.wait_ge(t_ready, j)
                    if cc == 0:
                        pe.wait_ge(seg_loaded[slot][SEGS[k]], loads)
                    last = add_t(slot, k, cc, PB, seg_done if cc == PB - 1 else None)
                    if u == len(UNITS) - 1:
                        last.then_inc(t_summed, 1)
                    if u > 0:
                        add(u - 1)
                add(len(UNITS) - 1)
                combine_t(j)

            for k in range(NS):
                pe.wait_ge(e_made, k + 1)
                pe.wait_ge(seg_loaded[0][SEGS[k]], DMA)
                last = add_t(0, k, 0, 1)
            last.then_inc(t_summed, 1)
            pe.wait_ge(zeroed, 1)
            for s in SEGS:
                nc.tensor.matmul(h_bank[s][:, :], zeros[:, 0:P], zeros[:, :], start=True, stop=False,
                                 skip_group_check=True)
            combine_t(0)
            layer0_panel(1, 1, DMA)
            with pe.Fori(0, NJ // 2 - 1) as two:
                layer0_panel(0, two * 2 + 2, (two + 2) * DMA, two)
                layer0_panel(1, two * 2 + 3, (two + 2) * DMA, two)

            def turn_h(n, s):
                pe.wait_ge(h_copied, n + 1)
                if n >= 1:
                    pe.wait_ge(y_copied, n)
                for bank, matrix in ((h_bank[s], centre), (t_bank, centre_gamma)):
                    for c in range(GB):
                        last = nc.tensor.matmul(bank[:, c * P:(c + 1) * P], scratch[:, n % 2, c * P:(c + 1) * P],
                                                matrix[:, :], start=True, stop=True)
                last.then_inc(h_turned, 1)

            pe.wait_ge(weights_made, 6)
            pe.wait_ge(t_ready, NJ)
            before = (NJ - 1) * len(ITEMS)
            for u, (k, cc) in enumerate([*UNITS, (NS, 0), (NS, 1)]):
                if k < NS:
                    turn_blocks(1, (k, cc), before)
                if cc == 1 and k >= 1:
                    turn_h(k - 1, SEGS[k - 1])
                if 0 < u <= len(UNITS):
                    done, chunk = UNITS[u - 1]
                    add_h(1, (done, chunk), before, chunk == PB - 1)
                    if u == 1:
                        pe.wait_ge(t_quartered, NG)
                    if done < TILED:
                        for c in range(chunk * GB // PB, (chunk + 1) * GB // PB):
                            add_h_tile(done, c, T1 - TILED + done, c == GB - 1)

            def add_tile(t, place, c, parity, first, last_tile, columns, middle=None):
                pe.wait_ge(tile_turned, t + 1 + RAW)
                for i in range(GB):
                    if i == GB // 2 and middle:
                        middle()
                    last = nc.tensor.matmul(sum_bank[parity][:, :], terms[:, c * GB + i, columns],
                                            turned[place][:, i * BANK:(i + 1) * BANK],
                                            start=(first and i == 0), stop=(last_tile and i == GB - 1))
                last.then_inc(tile_used, 1)

            def add_tile_halves(t, place, c, parity, first, last_tile, middle=None):
                pe.wait_ge(tile_turned, t + 1 + RAW)
                for i in range(GB):
                    if i == GB // 2 and middle:
                        middle()
                    odd = i % 2
                    last = nc.tensor.matmul(sum_bank[parity][H * odd:H * (odd + 1), :],
                                            terms[:, c * GB + i, 2 * H:3 * H],
                                            turned[place][:, i * BANK:(i + 1) * BANK],
                                            start=(first and i < 2), stop=(last_tile and i >= GB - 2))
                last.then_inc(tile_used, 1)

            def turn_row(n, parity, width):
                pe.wait_ge(row_copied, n + 1)
                for c in range(GB):
                    last = nc.tensor.transpose(back_bank[:, c * width:(c + 1) * width],
                                               scratch[0:width, parity, c * P:(c + 1) * P], ident[0:width, 0:width])
                last.then_inc(row_back, 1)

            def sweep1_row(row, parity, tile, first_row=False):
                for k, c in enumerate(DOWN):
                    if first_row and k % 2 == 0:
                        pe.wait_ge(normed, k // 2 + 1)
                    if k == 1 and not first_row:
                        pe.wait_ge(row_written, row)
                    middle = (lambda: turn_row(row - 1, 1 - parity, PH)) if k == 0 and not first_row else None
                    add_tile(tile + k, (parity * NG + k) % TURNED, c, parity, k == 0, k == NG - 1,
                             slice(0, PH), middle)

            pe.wait_ge(zeroed, 2)
            sweep1_row(0, 0, T1, first_row=True)
            sweep1_row(1, 1, T1 + NG)
            with pe.Fori(1, NG // 2) as two:
                for r in range(2):
                    sweep1_row(two * 2 + r, r, two * PAIR + (T1 + r * NG))

            t = T2
            for i, g in enumerate(DOWN):
                mine = [c for row, c in sweep2 if row == g]
                before = ROWS1 + i - 1
                if i == 0:
                    turn_row(before, 1, PH)
                for k, c in enumerate(mine):
                    if k == len(mine) - 1:
                        pe.wait_ge(row_written, before + 1)
                    middle = (lambda: turn_row(before, 1 - i % 2, H)) if k == 0 and i > 0 else None
                    add_tile(t, late_slots(t - T2)[3], c, i % 2, k == 0, k == len(mine) - 1, slice(H, 3 * H), middle)
                    t += 1

            def turn_p(i, g):
                for c in range(GB):
                    last = nc.tensor.transpose(pt_bank[0:H, c * P:(c + 1) * P], terms[:, g * GB + c, 0:H], ident[:, :])
                last.then_inc(pt_turned, 1)

            def output(i, g):
                at = slice(g * BANK, (g + 1) * BANK)
                pe.wait_ge(row_copied, ROWS2 + i + 1)
                pe.wait_ge(row_kept, ROWS2)
                pe.wait_ge(weights_made, 6)
                if i:
                    pe.wait_ge(o_copied, i)
                nc.tensor.matmul(o_bank[0:H, :], w_sums1[:, :], sums1[:, at], start=True, stop=False)
                nc.tensor.matmul(o_bank[H:PH, :], w_sums2[:, :], sums2[:, at], start=True, stop=False)
                nc.tensor.matmul(o_bank[0:H, :], w_sums3[:, :], scratch[:, i % 2, :], start=False, stop=True)
                pe.wait_ge(pt_copied, i + 1)
                nc.tensor.matmul(o_bank[H:PH, :], w_p[:, :], p_turned, start=False, stop=True).then_inc(o_summed, 1)

            def turn_output(i):
                pe.wait_ge(o_copied, i + 1)
                if i >= 2:
                    pe.wait_ge(out_taken, i - 1)
                for c in range(GB):
                    last = nc.tensor.transpose(out_bank[i % 2][:, c * P:(c + 1) * P], o_turned[:, c * P:(c + 1) * P],
                                               ident[:, :])
                last.then_inc(out_summed, 1)

            for i, g in enumerate(DOWN):
                for k in range(g + 1):
                    c = g - k
                    middle = None
                    if k == 0 and i == 0:
                        middle = lambda: turn_row(ROWS2 - 1, 1, H)
                    elif k == 0:
                        middle = lambda: turn_p(i - 1, DOWN[i - 1])
                    if i == 0 and k == g:
                        pe.wait_ge(row_written, ROWS2)
                    add_tile_halves(t, late_slots(t - T2)[3], c, i % 2, k == 0, k == g, middle)
                    t += 1
                    if k == 0 and i > 0:
                        output(i - 1, DOWN[i - 1])
                    if k == min(1, g) and i > 0:
                        turn_output(i - 1)
            turn_p(NG - 1, DOWN[-1])
            output(NG - 1, DOWN[-1])
            turn_output(NG - 1)


_INS = ["x", "adj", "L0_gnn_W_u", "L0_gnn_diag_u", "L0_gnn_par_u", "L0_gnn_W_i", "L0_gnn_diag_i", "L0_gnn_par_i",
        "L0_gnn_ln_gamma", "L0_gnn_ln_beta", "L1_gnn_weight", "L1_gnn_bias"]


def kernel(**inputs):
    import numpy as _np
    import concourse.bacc as _bacc
    from concourse.bass_utils import run_bass_kernel_spmd as _run

    nc = _bacc.Bacc("TRN2", target_bir_lowering=False, num_devices=1)
    arrays, args = {}, []
    for name in _INS:
        a = _np.ascontiguousarray(inputs[name])
        arrays[f"in_{name}"] = a
        args.append(nc.dram_tensor(f"in_{name}", a.shape, mybir.dt.from_np(a.dtype), kind="ExternalInput").ap())
    shape = inputs["x"].shape
    args.append(nc.dram_tensor("out_0", shape, F32, kind="ExternalOutput").ap())
    resnorm_chebyshev(nc, *args)
    r = _run(nc, [arrays], core_ids=[0])
    return r.results[0]["out_0"]
```

```python
from contextlib import ExitStack

import concourse.bass as bass
from concourse import mybir

F32 = mybir.dt.float32
BF16 = mybir.dt.bfloat16
ALU = mybir.AluOpType
ACT = mybir.ActivationFunctionType
AX = mybir.AxisListType.X

P = 128
H = 64
PH = 2 * H
Q32 = 32
BANK = 512
PW = 256
PB = PW // P
NQ = P // Q32
EPS = 1e-5
RAW = 4
TURNED = 2
MORE_RAW = 3
MORE_TURNED = 2
AT = 2
DMA = 16


def resnorm_chebyshev(nc, x, adj, W_u, diag_u, par_u, W_i, diag_i, par_i, gamma, beta, weight, bias, out):
    N = adj.shape[0]
    NU = diag_u.shape[0]
    NB = N // P
    NG = N // BANK
    NJ = N // PW
    GB = BANK // P
    NS = NG // 2
    SB = 2 * GB
    UB = NU // P
    assert x.shape[1] == H and N % (2 * BANK) == 0 and NU % P == 0 and NG % 2 == 0 and NJ % 2 == 0
    assert (2 * NG) % RAW == 0 and (2 * NG) % TURNED == 0 and UB % 2 == 0

    with ExitStack() as ctx:
        def sb(name, shape, dt=F32):
            return ctx.enter_context(nc.sbuf_tensor(name, shape, dt))

        def sem(name):
            return ctx.enter_context(nc.semaphore(name))

        panel_size = NB * PW
        shared = sb("shared", [P, 2 * panel_size + NB * H + PB * SB * P])
        panels = [shared[:, k * panel_size:(k + 1) * panel_size].rearrange("p (b c) -> p b c", c=PW)
                  for k in range(2)]
        at = 2 * panel_size
        e = shared[:, at:at + NB * H].rearrange("p (b f) -> p b f", f=H)
        at += NB * H
        low_turned = shared[:, at:at + PB * SB * P].rearrange("p (cc b r) -> p b cc r", cc=PB, r=P)
        sums1 = shared[:, 0:N]
        sums2 = shared[:, N:2 * N]
        norm_squares = [shared[:, N + n * BANK:N + (n + 1) * BANK] for n in range(NS)]
        norm_terms = [shared[:, N + (NS + n) * BANK:N + (NS + n + 1) * BANK] for n in range(NS)]
        at = 2 * N
        r_start = shared[:, at:at + NB * H].rearrange("p (k f) -> p k f", f=H)
        at += NB * H
        p_turned = shared[0:H, at:at + BANK]
        at += BANK
        o_turned = shared[:, at:at + BANK]
        at += BANK

        terms = sb("terms", [P, NB, 3 * H])
        xq = sb("xq", [P, NB, H])
        tile_size = GB * BANK
        raw_base = sb("raw", [P, RAW * tile_size])
        turned_base = sb("turned", [P, TURNED * tile_size])
        raw = [raw_base[:, k * tile_size:(k + 1) * tile_size] for k in range(RAW)]
        turned = [turned_base[:, k * tile_size:(k + 1) * tile_size] for k in range(TURNED)]
        more = [shared[:, at + k * tile_size:at + (k + 1) * tile_size] for k in range(MORE_RAW + MORE_TURNED)]
        raw += [*more[:MORE_RAW], xq.rearrange("p k f -> p (k f)")[:, 0:tile_size]]
        turned += more[MORE_RAW:]
        ident = sb("ident", [P, P])
        centre = sb("centre", [P, P])
        centre_gamma = sb("centre_gamma", [P, P])
        both = sb("both", [P, H])
        zeros = sb("zeros", [P, BANK], BF16)
        t_sum = sb("t_sum", [P, PW])
        t_cols = sb("t_cols", [P, 2, PB * H])
        t_quart = sb("t_quart", [P, GB * H])
        scratch = sb("scratch", [P, 4, BANK])
        at_turned = [scratch[:, 2 + k, :] for k in range(AT)]
        squares = sb("squares", [P, BANK])
        stats = sb("stats", [P, 3, 2 * GB])
        w_pair = sb("w_pair", [P, 2, PH])
        par = sb("par", [P, 4])
        scales = sb("scales", [P, 2])
        diag_rows = sb("diag_rows", [NB, P])
        diag = sb("diag", [P, NB])
        w = sb("w", [P, 4, H])
        w_sums1 = sb("w_sums1", [P, H])
        w_sums2 = sb("w_sums2", [P, H])
        w_sums3 = sb("w_sums3", [P, H])
        w_p = sb("w_p", [H, H])
        rows = sb("rows", [P, 3, H])
        bias_column = sb("bias_column", [P, 1])

        banks = [ctx.enter_context(nc.psum_tensor(f"bank{i}", [P, BANK], F32)) for i in range(8)]
        h_bank = banks[0:NS]
        t_bank = banks[5]
        turn_bank = banks[6:8]
        sum_bank = banks[6:8]
        back_bank = banks[5]
        odd_bank = banks[4]
        pt_bank = banks[4]
        o_bank = banks[3]
        out_bank = banks[1:3]

        consts_loaded = sem("consts_loaded")
        x_loaded = sem("x_loaded")
        xq_loaded = sem("xq_loaded")
        xq_made = sem("xq_made")
        late_loaded = sem("late_loaded")
        zeroed = sem("zeroed")
        ident_made = sem("ident_made")
        diag_turned = sem("diag_turned")
        x_scaled = sem("x_scaled")
        x_turned = sem("x_turned")
        x_copied = sem("x_copied")
        e_product = sem("e_product")
        e_made = sem("e_made")
        seg_loaded = [[sem(f"seg_loaded{k}_{s}") for s in range(NS)] for k in range(2)]
        seg_done = sem("seg_done")
        at_made = sem("at_made")
        at_copied = sem("at_copied")
        at_used = sem("at_used")
        low_made = sem("low_made")
        low_used = sem("low_used")
        t_summed = sem("t_summed")
        t_copied = sem("t_copied")
        t_combined = sem("t_combined")
        t_ready = sem("t_ready")
        t_quartered = sem("t_quartered")
        h_copied = sem("h_copied")
        h_turned = sem("h_turned")
        y_copied = sem("y_copied")
        normed = sem("normed")
        dve_step = sem("dve_step")
        pool_step = sem("pool_step")
        var_made = sem("var_made")
        root_made = sem("root_made")
        w_cleared = sem("w_cleared")
        raw_loaded = [sem(f"raw_loaded{k}") for k in range(len(raw))]
        tile_turned = sem("tile_turned")
        tile_used = sem("tile_used")
        fold_cleared = sem("fold_cleared")
        odd_copied = sem("odd_copied")
        row_copied = sem("row_copied")
        diag_used = sem("diag_used")
        u_copied = sem("u_copied")
        u_back = sem("u_back")
        u_written = sem("u_written")
        row_kept = sem("row_kept")
        row_back = sem("row_back")
        row_written = sem("row_written")
        weights_made = sem("weights_made")
        xq_step = sem("xq_step")
        pt_turned = sem("pt_turned")
        pt_copied = sem("pt_copied")
        o_summed = sem("o_summed")
        o_copied = sem("o_copied")
        out_summed = sem("out_summed")
        out_taken = sem("out_taken")
        out_made = sem("out_made")
        out_stored = [sem(f"out_stored{k}") for k in range(2)]

        SEGS = [NS - 1 - k for k in range(NS)]
        DOWN = [NG - 1 - k for k in range(NG)]

        TILED = NS - 1
        ITEMS = TILED * PB
        T1 = TILED * NG
        assert TILED == RAW and T1 % RAW == 0 and TILED // 2 * GB <= ITEMS and ITEMS % AT == 0

        sweep2 = [(g, c) for g in DOWN for c in range(NG - 1, g, -1)]
        ROWS3 = [g for k in range(NG // 2) for g in (NG - 1 - k, k)]
        sweep3 = [(g, c) for g in ROWS3 for c in range(g, -1, -1)]
        FINISH = 4
        END3 = [sum(g + 1 for g in ROWS3[:i + 1]) for i in range(NG)]
        PAIR = 2 * NG
        first_rows = [(g, DOWN[k + i]) for k in range(0, NG, 2) for g in range(2) for i in range(2)]
        T2 = T1 + NG * NG
        late_tiles = sweep2 + sweep3
        row_end = {n: T1 + ((n + 1) * NG if n else PAIR - 2) for n in range(NG)}
        ROWS1, ROWS2 = NG, 2 * NG - 1
        for n in range(ROWS1, ROWS2 + NG):
            row_end[n] = row_end[n - 1] + (n - ROWS1 + 1 if n < ROWS2 else ROWS3[n - ROWS2] + 1)

        def place1(g, c, n):
            return TURNED + g % 2 if g == c else n % TURNED

        def late_slots(n):
            found = []
            for base, count in ((RAW, len(raw)), (TURNED, TURNED + MORE_TURNED)):
                slot = n % count
                before = T2 // base if slot < base else 0
                last = T2 + n - count if n >= count else (T2 - base + slot if slot < base else None)
                found += [slot, before + n // count, last]
            return found

        def by_chunk(a, width):
            return a.rearrange("p (k f) -> p k f", f=width)

        def wide(a, count):
            return a.rearrange("p (k o) -> p k o", o=1).to_broadcast([P, count, H])

        def quarter(a, g, q):
            return a[BANK * g + P * q:BANK * g + P * (q + 1), :].rearrange("(c j) f -> j c f", j=Q32)

        def chunk_order(a):
            return a.rearrange("p (q c j) -> p c q j", q=NQ, j=Q32)

        def split(a):
            return a.rearrange("p (c q j) -> p c q j", q=NQ, j=Q32)

        block = ctx.enter_context(nc.Block())

        @block.sync
        def _(sp):
            sp.dma_start(diag_rows[0:UB, :], diag_u.rearrange("(b p) -> b p", p=P)).then_inc(consts_loaded, DMA)
            sp.dma_start(diag_rows[UB:NB, :], diag_i.rearrange("(b p) -> b p", p=P)).then_inc(consts_loaded, DMA)
            sp.dma_start(e[:, :, :], x.rearrange("(b p) f -> p b f", p=P)).then_inc(x_loaded, DMA)
            sp.wait_ge(w_cleared, 1)
            for k, a in enumerate((W_u, W_i)):
                for half in range(2):
                    rows_of = slice(H * half, H * (half + 1))
                    sp.dma_start(w_pair[rows_of, k, rows_of], a).then_inc(consts_loaded, DMA)
            for k, a in enumerate((par_u, par_i)):
                sp.dma_start(par[:, 2 * k:2 * k + 2], a.rearrange("(o n) -> o n", o=1).to_broadcast([P, 2]))\
                    .then_inc(consts_loaded, DMA)

            seg_rows = adj.rearrange("(s b p) c -> s p b c", p=P, b=SB)
            block_rows = adj.rearrange("(b i) c -> i b c", i=Q32)
            tile_rows = adj.rearrange("(g b i) c -> g i b c", b=BANK // Q32, i=Q32)

            def load_tile(slot, last, first_block, column):
                if last is not None:
                    sp.wait_ge(tile_turned, last + 1 + RAW)
                for q in reversed(range(NQ)):
                    sp.dma_start(raw[slot][Q32 * q:Q32 * (q + 1), :].rearrange("p (b c) -> p b c", c=P),
                                 block_rows[:, bass.ds(first_block, BANK // Q32), column + P * q:column + P * (q + 1)])\
                        .then_inc(raw_loaded[slot], DMA)

            def load_layer0_tile(k, last, column):
                if last is not None:
                    sp.wait_ge(tile_turned, last + 1 + RAW)
                for q in range(NQ):
                    sp.dma_start(raw[k][Q32 * q:Q32 * (q + 1), :].rearrange("p (b c) -> p b c", c=P),
                                 tile_rows[2 * SEGS[k] + 1][:, :, bass.ds(column + P * q, P)])\
                        .then_inc(raw_loaded[k], DMA)

            def load_panel(slot, uses, column, tiles=(), first=False):
                for k, s in enumerate(SEGS):
                    if k < TILED:
                        sp.wait_ge(seg_done, (uses * 2 + slot) * TILED + (k + 1))
                    elif not first:
                        sp.wait_ge(low_made, uses * 2 + (slot - 1))
                    sp.dma_start(panels[slot][:, s * SB:(s + 1) * SB, :], seg_rows[s][:, :, bass.ds(column, PW)])\
                        .then_inc(seg_loaded[slot][s], DMA)
                    if tiles and k in (1, 3):
                        load_layer0_tile(*tiles[k // 2])

            load_panel(0, 0, 0, first=True)
            load_panel(1, 0, PW, [(0, None, 0), (1, None, 0)], first=True)
            with sp.Fori(2, NJ // 2 + 1) as pair:
                end = sp.snap(pair * BANK)
                for slot in range(2):
                    load_panel(slot, pair - 1, end + (slot - 2) * PW,
                               [((2 * slot + 2 + n) % RAW, (pair - 1) * TILED + (2 * slot - 2 + n - RAW),
                                 end + (slot - 2) * BANK) for n in range(2)])
            for n in range(2, TILED):
                load_layer0_tile(n, T1 - TILED + n - RAW, (NG - 1) * BANK)

            for n, (g, c) in enumerate(first_rows):
                load_tile(n % RAW, T1 + n - RAW, g * (BANK // Q32), c * BANK)
            with sp.Fori(1, NG // 2) as two:
                for n in range(PAIR):
                    load_tile(n % RAW, two * PAIR + (T1 + n - RAW), (two * 2 + n // NG) * (BANK // Q32),
                              DOWN[n % NG] * BANK)
            for n, (g, c) in enumerate(late_tiles):
                slot, _, last = late_slots(n)[0:3]
                load_tile(slot, last, g * (BANK // Q32), c * BANK)

        @block.gpsimd
        def _(pool):
            nc.gpsimd.memset(ident[:, :], 0.0).then_inc(pool_step, 1)
            nc.gpsimd.memset(both[:, :], 0.0).then_inc(pool_step, 1)
            pool.wait_ge(pool_step, 2)
            nc.gpsimd.affine_select(out=ident[:, :], in_=ident[:, :], compare_op=ALU.not_equal, fill=1.0,
                                    base=0, pattern=[[-1, P]], channel_multiplier=1).then_inc(ident_made, 1)
            nc.gpsimd.affine_select(out=both[:, :], in_=both[:, :], compare_op=ALU.not_equal, fill=1.0,
                                    base=0, pattern=[[-1, H]], channel_multiplier=1).then_inc(pool_step, 1)
            pool.wait_ge(pool_step, 3)
            nc.gpsimd.affine_select(out=both[:, :], in_=both[:, :], compare_op=ALU.not_equal, fill=1.0,
                                    base=-H, pattern=[[-1, H]], channel_multiplier=1).then_inc(ident_made, 1)
            nc.gpsimd.memset(zeros[:, :], 0.0).then_inc(zeroed, 1)
            pool.wait_ge(t_ready, 1)
            for k, a in enumerate((gamma, beta, bias)):
                pool.dma_start(rows[:, k, :], a.rearrange("(o f) -> o f", o=1).to_broadcast([P, H]))\
                    .then_inc(late_loaded, DMA)
            for k in range(2):
                pool.dma_start(w[H * k:H * (k + 1), :, :], weight.rearrange("k i o -> i k o"))\
                    .then_inc(late_loaded, DMA)
            for g in range(NG):
                for q in range(NQ):
                    pool.dma_start(xq[Q32 * q:Q32 * (q + 1), g * GB:(g + 1) * GB, :], quarter(x, g, q))\
                        .then_inc(xq_loaded, DMA)
            nc.gpsimd.memset(terms[:, :, H:3 * H], 0.0).then_inc(zeroed, 1)
            pool.wait_ge(late_loaded, DMA * 5)
            pool.wait_ge(xq_loaded, DMA * NG * NQ)
            nc.gpsimd.tensor_tensor(out=xq[:, :, :], in0=xq[:, :, :], in1=xq[:, :, :], op=ALU.add)\
                .then_inc(pool_step, 1)
            pool.wait_ge(pool_step, 4)
            nc.gpsimd.tensor_tensor(out=xq[:, :, :], in0=xq[:, :, :],
                                    in1=rows[:, 1:2, :].to_broadcast([P, NB, H]), op=ALU.add).then_inc(xq_made, 1)
            for n, g in enumerate(ROWS3):
                pool.wait_ge(out_made, n + 1)
                for q in range(NQ):
                    y = scratch[Q32 * q:Q32 * (q + 1), 2 + n % 2, 0:GB * H]
                    pool.dma_start(quarter(out, g, q), by_chunk(y, H))\
                        .then_inc(out_stored[n % 2], DMA)
            for k in range(2):
                pool.wait_ge(out_stored[k], DMA * NQ * (NG // 2))

        @block.vector
        def _(dve):
            steps = [0]

            def chain(instruction):
                steps[0] += 1
                instruction.then_inc(dve_step, 1)
                dve.wait_ge(dve_step, steps[0])

            roots = [0]

            def remove_mean(a, count):
                mean = stats[:, 0, 0:count]
                chain(nc.vector.tensor_reduce(out=mean, in_=a, axis=AX, op=ALU.add))
                chain(nc.vector.tensor_scalar(mean, mean, 1.0 / H, None, ALU.mult))
                chain(nc.vector.tensor_tensor(a, a, wide(mean, count), ALU.subtract))

            def variance(squares_of, count):
                var = stats[:, 0, 0:count]
                chain(nc.vector.tensor_reduce(out=var, in_=squares_of, axis=AX, op=ALU.add))
                nc.vector.tensor_scalar(var, var, 1.0 / H, EPS, ALU.mult, ALU.add).then_inc(var_made, 1)

            def inverse_root(count):
                inv = stats[:, 2, 0:count]
                roots[0] += 1
                dve.wait_ge(root_made, roots[0])
                chain(nc.vector.reciprocal(inv, stats[:, 1, 0:count]))
                return wide(inv, count)

            dve.sem_inc(tile_turned, RAW)
            nc.vector.memset(w_pair[:, :, :], 0.0).then_inc(w_cleared, 1)
            dve.wait_ge(consts_loaded, DMA * 8)
            chain(nc.vector.tensor_tensor(scales[:, 0:1], par[:, 0:1], par[:, 1:2], ALU.mult))
            chain(nc.vector.tensor_tensor(scales[:, 1:2], par[:, 2:3], par[:, 3:4], ALU.mult))
            for k in range(2):
                chain(nc.vector.tensor_scalar(w_pair[:, k, :], w_pair[:, k, :], scales[:, k:k + 1], None, ALU.mult))
            dve.wait_ge(diag_turned, 1)
            chain(nc.vector.tensor_copy(diag[:, :], t_bank[:, 0:NB]))
            dve.wait_ge(x_loaded, DMA)
            for s in SEGS:
                b = slice(s * SB, (s + 1) * SB)
                nc.vector.tensor_tensor(xq[:, b, :], e[:, b, :], wide(diag[:, b], SB), ALU.mult).then_inc(x_scaled, 1)
            for n, s in enumerate(SEGS):
                b = slice(s * SB, (s + 1) * SB)
                dve.wait_ge(e_product, n + 1)
                nc.vector.tensor_tensor(e[:, b, :], by_chunk(banks[n % 2][:, :], H), e[:, b, :], ALU.add)\
                    .then_inc(e_made, 1)

            def turn_tile(slot, loads, place, last):
                dve.wait_ge(raw_loaded[slot], loads)
                if last is not None:
                    dve.wait_ge(tile_used, last + 1 + TURNED)
                nc.vector.transpose(turned[place].rearrange("p (c b i) -> p b c i", c=GB, i=Q32),
                                    raw[slot].rearrange("p (b c i) -> p b c i", c=GB, i=Q32))\
                    .then_inc(tile_turned, 1)

            def turn_low(slot, j, quadrants=range(NQ)):
                if 0 in quadrants:
                    dve.wait_ge(low_used, j)
                low = panels[slot][:, SEGS[-1] * SB:(SEGS[-1] + 1) * SB, :].rearrange("p b (cc c) -> p b cc c", c=P)
                for q in quadrants:
                    for c in range(NQ):
                        last = nc.vector.transpose(
                            low_turned[Q32 * c:Q32 * (c + 1), :, :, Q32 * q:Q32 * (q + 1)],
                            low[Q32 * q:Q32 * (q + 1), :, :, Q32 * c:Q32 * (c + 1)])
                if NQ - 1 in quadrants:
                    last.then_inc(low_made, 1)

            def quarter_t(m):
                for q in range(NQ):
                    for c in range(GB):
                        part = t_cols[Q32 * c:Q32 * (c + 1), q // PB, q % PB * H:(q % PB + 1) * H]
                        last = nc.vector.tensor_copy(t_quart[Q32 * q:Q32 * (q + 1), c * H:(c + 1) * H], part)
                last.then_inc(t_quartered, 1)

            def center_xq(g):
                part = xq[:, bass.ds(g * GB, GB), :]
                mean = stats[:, 0, 0:GB]
                dve.wait_ge(xq_made, 1)
                nc.vector.tensor_reduce(out=mean, in_=part, axis=AX, op=ALU.add).then_inc(xq_step, 1)
                dve.wait_ge(xq_step, g * 3 + 1)
                nc.vector.tensor_scalar(mean, mean, 1.0 / H, None, ALU.mult).then_inc(xq_step, 1)
                dve.wait_ge(xq_step, g * 3 + 2)
                nc.vector.tensor_tensor(part, part, wide(mean, GB), ALU.subtract).then_inc(xq_step, 1)
                dve.wait_ge(xq_step, g * 3 + 3)

            def beside_panel(slot, j, m, tile, groups):
                dve.wait_ge(t_ready, j)
                if m is not None:
                    quarter_t(m)
                turn_low(slot, j)
                for n in range(2):
                    turn_tile((tile + n) % RAW, groups * (DMA * NQ) + DMA * NQ * ((tile + n) // RAW + 1),
                              n % TURNED, groups * TILED + (tile + n - TURNED))

            beside_panel(0, 1, None, 0, 0)
            with dve.Fori(0, NG - 1 - NG // 2) as m:
                beside_panel(1, m * 2 + 2, m, 2, m)
                beside_panel(0, m * 2 + 3, None, 4, m)

            dve.wait_ge(late_loaded, DMA * 5)
            dve.wait_ge(ident_made, 2)
            chain(nc.vector.tensor_copy(centre[:, :], ident[:, :]))
            remove_mean(by_chunk(centre[:, :], H), 2)
            chain(nc.vector.tensor_tensor(by_chunk(centre_gamma[:, :], H), by_chunk(centre[:, :], H),
                                          rows[:, 0:1, :].to_broadcast([P, 2, H]), ALU.mult))
            remove_mean(by_chunk(centre_gamma[:, :], H), 2)
            chain(nc.vector.tensor_tensor(w[:, 0, :], w[:, 0, :], both[:, :], ALU.add))
            remove_mean(w[:, :, :], 4)
            remove_mean(rows[:, 2:3, :], 1)
            chain(nc.vector.memset(bias_column[:, :], 0.0))
            chain(nc.vector.tensor_tensor(squares[0:H, 0:H], rows[0:H, 2, :], both[0:H, :], ALU.mult))
            chain(nc.vector.tensor_reduce(out=bias_column[0:H, :], in_=squares[0:H, 0:H], axis=AX, op=ALU.add))
            lo, hi = slice(0, H), slice(H, P)
            nc.vector.tensor_tensor(w_p[:, :], w[lo, 0, :], w[lo, 2, :], ALU.subtract).then_inc(weights_made, 1)
            nc.vector.tensor_tensor(w_sums1[lo, :], w[lo, 1, :], w[lo, 3, :], ALU.subtract).then_inc(weights_made, 1)
            nc.vector.tensor_scalar(w_sums1[hi, :], w[hi, 2, :], 2.0, None, ALU.mult).then_inc(weights_made, 1)
            nc.vector.tensor_scalar(w_sums2[lo, :], w[lo, 2, :], 2.0, None, ALU.mult).then_inc(weights_made, 1)
            nc.vector.tensor_scalar(w_sums2[hi, :], w[hi, 3, :], 2.0, None, ALU.mult).then_inc(weights_made, 1)
            nc.vector.tensor_scalar(w_sums3[:, :], w[:, 3, :], 2.0, None, ALU.mult).then_inc(weights_made, 1)

            with dve.Fori(NG - 1 - NG // 2, NG - 1) as m:
                beside_panel(1, m * 2 + 2, m, 2, m)
                beside_panel(0, m * 2 + 3, None, 4, m)
                for k in range(2):
                    center_xq(m * 2 + (k - 2 * (NG - 1 - NG // 2)))
            dve.wait_ge(t_ready, NJ)
            quarter_t(NG - 1)
            turn_low(1, NJ, range(NQ // 2))
            for t in (T1 - 2, T1 - 1):
                turn_tile(t % RAW, DMA * NQ * (t // RAW + 1), t % TURNED, t - TURNED)
            turn_low(1, NJ, range(NQ // 2, NQ))

            def norm_step(n, step):
                y, sq = by_chunk(norm_terms[n], H), by_chunk(squares[:, :], H)
                k = slice(2 * SEGS[n] * GB, 2 * (SEGS[n] + 1) * GB)
                if step == 0:
                    dve.wait_ge(y_copied, n + 1)
                    variance(by_chunk(norm_squares[n], H), 2 * GB)
                elif step == 1:
                    chain(nc.vector.tensor_tensor(y, y, inverse_root(2 * GB), ALU.mult))
                elif step == 2:
                    chain(nc.vector.tensor_tensor(y, y, xq[:, k, :], ALU.add))
                    chain(nc.vector.tensor_tensor(sq, y, y, ALU.mult))
                elif step == 3:
                    variance(sq, 2 * GB)
                else:
                    nc.vector.tensor_tensor(terms[:, k, 0:H], y, inverse_root(2 * GB), ALU.mult).then_inc(normed, 1)

            def sweep1_tile(n, g, c):
                t = T1 + n
                if g == c and g >= 2:
                    dve.wait_ge(diag_used, g - 1)
                turn_tile(t % RAW, DMA * NQ * (t // RAW + 1), place1(g, c, n), t - TURNED)

            steps_left = [(n, step) for n in range(NS) for step in range(5)]

            def norm_steps(count):
                for _ in range(count):
                    norm_step(*steps_left.pop(0))

            norm_steps(5)
            sweep1_tile(0, *first_rows[0])
            norm_steps(3)
            sweep1_tile(1, *first_rows[1])
            norm_steps(2)
            for n in range(2, PAIR):
                sweep1_tile(n, *first_rows[n])
                norm_steps(min(len(steps_left), 2 if n == 2 else 1))

            nc.vector.memset(squares[0:H, :], 0.0).then_inc(fold_cleared, 1)

            def write_q(g):
                dve.wait_ge(row_back, g + 1)
                nc.vector.tensor_copy(terms[:, g * GB:(g + 1) * GB, H:2 * H], by_chunk(back_bank[:, :], PH)[:, :, 0:H])\
                    .then_inc(row_written, 1)

            def write_u(g):
                dve.wait_ge(u_back, g + 1)
                k = slice(g * GB, (g + 1) * GB)
                nc.vector.scalar_tensor_tensor(out=terms[:, k, 2 * H:3 * H] if g == NG - 1 else r_start[:, k, :],
                                               in0=by_chunk(back_bank[:, :], PH)[:, :, H:PH], scalar=2.0,
                                               in1=terms[:, k, 0:H], op0=ALU.mult, op1=ALU.subtract)\
                    .then_inc(u_written, 1)

            def write_r(n, g):
                dve.wait_ge(row_back, n + 1)
                k = slice(g * GB, (g + 1) * GB)
                nc.vector.scalar_tensor_tensor(out=terms[:, k, 2 * H:3 * H], in0=by_chunk(back_bank[:, 0:GB * H], H),
                                               scalar=2.0, in1=r_start[:, k, :], op0=ALU.mult, op1=ALU.add)\
                    .then_inc(row_written, 1)

            write_q(0)
            for g in range(2, NG):
                for k, c in enumerate(DOWN):
                    sweep1_tile(g * NG + k, g, c)
                    if g == 2 and k == 0:
                        write_u(0)
                    if k == 1:
                        write_q(g - 1)
                    if k == 6:
                        write_u(g - 1)

            def late_tile(n):
                slot, uses, _, place, _, last = late_slots(n)
                if last is None and place >= TURNED:
                    dve.wait_ge(diag_used, NG - TURNED + 1 + place - TURNED)
                turn_tile(slot, DMA * NQ * (uses + 1), place, last)

            def finish(n):
                y, sq = by_chunk(scratch[:, 2 + n % 2, 0:GB * H], H), by_chunk(squares[:, 0:GB * H], H)
                if n >= 2:
                    dve.wait_ge(out_stored[n % 2], DMA * NQ * (n // 2))
                dve.wait_ge(out_summed, n + 1)
                halves = by_chunk(out_bank[n % 2][:, :], PH)
                chain(nc.vector.tensor_copy(y, halves[:, :, 0:H]))
                nc.vector.tensor_tensor(y, halves[:, :, H:PH], y, ALU.add).then_inc(out_taken, 1)
                dve.wait_ge(out_taken, n + 1)
                chain(nc.vector.tensor_tensor(sq, y, y, ALU.mult))
                variance(sq, GB)
                nc.vector.tensor_tensor(y, y, inverse_root(GB), ALU.mult).then_inc(out_made, 1)

            n = 0
            for i, g in enumerate(DOWN[1:]):
                for k in range(i + 1):
                    late_tile(n)
                    if n == TURNED - 1:
                        write_q(NG - 1)
                    if n == TURNED:
                        write_u(NG - 1)
                    if i > 0 and k == min(i, 3):
                        write_r(ROWS1 + i - 1, g + 1)
                    n += 1
            for t in range(len(sweep3)):
                late_tile(n)
                n += 1
                if t == 4:
                    write_r(ROWS2 - 1, DOWN[-1])
                if t - FINISH in END3:
                    finish(END3.index(t - FINISH))
            finish(NG - 1)

        @block.scalar
        def _(act):
            for n in range(NS):
                act.wait_ge(x_turned, n + 1)
                if n >= 2:
                    act.wait_ge(e_product, n - 1)
                nc.scalar.copy(scratch[:, n % 2, :], turn_bank[n % 2][:, :]).then_inc(x_copied, 1)

            act.sem_inc(at_copied, 2)

            def copy_turned(i, before):
                act.wait_ge(at_made, before + (i + 1))
                act.wait_ge(at_used, before + (i + 1))
                nc.scalar.copy(at_turned[i % AT], turn_bank[i % 2][:, :]).then_inc(at_copied, 1)

            def keep_t(slot, j):
                act.wait_ge(t_summed, j + 1)
                nc.scalar.copy(t_sum[:, :], t_bank[:, 0:PW]).then_inc(t_copied, 1)
                act.wait_ge(t_combined, j + 1)
                nc.scalar.copy(t_cols[:, slot, :], t_bank[:, PW:PW + PB * H]).then_inc(t_ready, 1)

            def layer0_panel(slot, j):
                for i in range(ITEMS):
                    copy_turned(i, (j - 1) * ITEMS)
                keep_t(slot, j)

            keep_t(0, 0)
            layer0_panel(1, 1)
            with act.Fori(1, NJ // 2) as two:
                layer0_panel(0, two * 2)
                layer0_panel(1, two * 2 + 1)

            def take_h(n, s):
                if n < TILED:
                    act.wait_ge(at_used, AT + (NJ - 1) * ITEMS + (n + 1) * PB)
                    act.wait_ge(tile_used, TURNED + T1 - TILED + n + 1)
                else:
                    act.wait_ge(low_used, NJ + 1)
                nc.scalar.copy(split(scratch[:, n % 2, :]), chunk_order(h_bank[s][:, :])).then_inc(h_copied, 1)

            def take_y(n, s):
                act.wait_ge(h_turned, n + 1)
                nc.scalar.activation(norm_squares[n].rearrange("p (g c f) -> p c g f", g=2, f=H),
                                     h_bank[s][:, :].rearrange("p (c g f) -> p c g f", g=2, f=H), ACT.Square)
                nc.scalar.copy(norm_terms[n].rearrange("p (g c f) -> p c g f", g=2, f=H),
                               t_bank[:, :].rearrange("p (c g f) -> p c g f", g=2, f=H)).then_inc(y_copied, 1)

            def root(n, count):
                act.wait_ge(var_made, n + 1)
                nc.scalar.activation(stats[:, 1, 0:count], stats[:, 0, 0:count], ACT.Sqrt).then_inc(root_made, 1)

            for k, s in enumerate(SEGS):
                for cc in range(PB):
                    if k < TILED:
                        copy_turned(k * PB + cc, (NJ - 1) * ITEMS)
                    if k >= 1:
                        (take_h, take_y)[cc](k - 1, SEGS[k - 1])
                    if (k, cc) == (NS - 1, PB - 1):
                        take_h(k, SEGS[k])
                    if k >= 3:
                        root(2 * k - 6 + cc, 2 * GB)
            take_y(NS - 1, SEGS[-1])
            for n in range(4, 2 * NS):
                root(n, 2 * GB)

            def take_row(n, parity, tiles, kept):
                act.wait_ge(tile_used, TURNED + tiles)
                nc.scalar.copy(split(scratch[:, parity, :]), chunk_order(sum_bank[parity][:, :]))\
                    .then_inc(row_copied, 1)
                if kept is not None:
                    act.wait_ge(row_copied, n + 1)
                    nc.scalar.copy(kept, scratch[:, parity, :]).then_inc(row_kept, 1)

            def take_q(g, parity, tiles):
                act.wait_ge(tile_used, TURNED + tiles)
                nc.scalar.copy(split(scratch[0:H, parity, :]), chunk_order(sum_bank[parity][0:H, :]))\
                    .then_inc(row_copied, 1)
                act.wait_ge(row_copied, g + 1)
                nc.scalar.copy(sums1[0:H, bass.ds(g * BANK, BANK)], scratch[0:H, parity, :]).then_inc(row_kept, 1)

            def take_u(g, parity):
                act.wait_ge(diag_used, g + 1)
                nc.scalar.copy(split(scratch[H:P, parity, :]), chunk_order(sum_bank[parity][H:P, :]))\
                    .then_inc(u_copied, 1)
                act.wait_ge(u_copied, g + 1)
                nc.scalar.copy(sums1[H:P, bass.ds(g * BANK, BANK)], scratch[H:P, parity, :]).then_inc(row_kept, 1)

            take_q(0, 0, row_end[0])
            take_u(0, 0)
            take_q(1, 1, row_end[1])
            with act.Fori(1, NG // 2) as two:
                for r in range(2):
                    take_u(two * 2 + (r - 1), 1 - r)
                    act.wait_ge(tile_used, (two * 2 + r) * (NG - 1) + (TURNED + T1 + NG))
                    nc.scalar.copy(squares[H:P, :], odd_bank[H:P, :]).then_inc(odd_copied, 1)
                    take_q(two * 2 + r, r, (two * 2 + r + 1) * NG + T1)
            take_u(NG - 1, 1)
            for i, g in enumerate(DOWN[1:]):
                take_row(ROWS1 + i, i % 2, row_end[ROWS1 + i], sums2[:, g * BANK:(g + 1) * BANK])
            def take_p(i):
                act.wait_ge(pt_turned, i + 1)
                nc.scalar.copy(p_turned, pt_bank[0:H, :]).then_inc(pt_copied, 1)

            def take_output(i):
                act.wait_ge(o_summed, 2 * (i + 1))
                nc.scalar.activation(o_turned, o_bank[:, :], ACT.Identity, bias=bias_column[:, :]).then_inc(o_copied, 1)

            for i in range(NG):
                done = [j for j in range(i) if END3[i - 1] <= END3[j] + FINISH - 2 < END3[i]]
                if i >= 1:
                    take_p(i - 1)
                    take_output(i - 1)
                if i == NG - 1:
                    take_p(i)
                for j in done:
                    root(2 * NS + j, GB)
                take_row(ROWS2 + i, (ROWS2 + i) % 2, row_end[ROWS2 + i], None)
            take_output(NG - 1)
            root(2 * NS + NG - 1, GB)

        @block.tensor
        def _(pe):
            pe.sem_inc(seg_done, 2 * TILED)
            pe.sem_inc(low_used, 1)
            pe.sem_inc(at_used, AT)
            pe.sem_inc(tile_used, TURNED)
            pe.wait_ge(ident_made, 2)
            pe.wait_ge(consts_loaded, DMA * 8)
            nc.tensor.transpose(t_bank[:, 0:NB], diag_rows[:, :], ident[0:NB, 0:NB]).then_inc(diag_turned, 1)

            def turn_x(n, s):
                pe.wait_ge(x_scaled, n + 1)
                if n >= 2:
                    pe.wait_ge(x_copied, n - 1)
                for c in range(SB // 2):
                    b = s * SB + 2 * c
                    last = nc.tensor.transpose(turn_bank[n % 2][:, c * P:(c + 1) * P],
                                               xq[:, b:b + 2, :].rearrange("p k f -> p (k f)"), ident[:, :])
                last.then_inc(x_turned, 1)

            def multiply_x(n, s):
                pe.wait_ge(x_copied, n + 1)
                if n >= 2:
                    pe.wait_ge(e_made, n - 1)
                for c in range(SB // 2):
                    items = int(s * SB + 2 * c >= UB)
                    last = nc.tensor.matmul(banks[n % 2][:, c * PH:(c + 1) * PH], scratch[:, n % 2, c * P:(c + 1) * P],
                                            w_pair[:, items, :], start=True, stop=True)
                last.then_inc(e_product, 1)

            turn_x(0, SEGS[0])
            for n, s in enumerate(SEGS):
                if n + 1 < NS:
                    turn_x(n + 1, SEGS[n + 1])
                multiply_x(n, s)

            def add_t(slot, k, half, half_count, signal=None):
                s = SEGS[k]
                last = None
                for b in range(half * SB // half_count, (half + 1) * SB // half_count):
                    odd = b % 2
                    if last and signal:
                        last.then_inc(signal, 1)
                        signal = None
                    last = nc.tensor.matmul(t_bank[H * odd:H * (odd + 1), 0:PW], e[:, s * SB + b, :],
                                            panels[slot][:, s * SB + b, :], start=(k == 0 and b < 2),
                                            stop=(k == NS - 1 and b >= SB - 2))
                return last

            UNITS = [(k, cc) for k in range(NS) for cc in range(PB)]

            def turn_blocks(slot, k, cc, before):
                i = k * PB + cc
                pe.wait_ge(at_copied, before + (i + 1))
                for b in range(GB):
                    last = nc.tensor.transpose(turn_bank[i % 2][:, b * P:(b + 1) * P],
                                               panels[slot][:, SEGS[k] * SB + b, cc * P:(cc + 1) * P], ident[:, :])
                last.then_inc(at_made, 1)

            def add_h(slot, k, cc, before, stop):
                i = k * PB + cc
                pe.wait_ge(at_copied, before + (i + 3))
                nc.tensor.matmul(h_bank[SEGS[k]][0:H, :], t_cols[:, slot, cc * H:(cc + 1) * H], at_turned[i % AT],
                                 start=False, stop=stop, skip_group_check=True).then_inc(at_used, 1)

            def add_h_low(slot, cc, j, stop):
                if cc == 0:
                    pe.wait_ge(low_made, j)
                for gg in range(2):
                    last = nc.tensor.matmul(h_bank[SEGS[-1]][H * gg:H * (gg + 1), :],
                                            t_cols[:, slot, cc * H:(cc + 1) * H],
                                            low_turned[:, gg * GB:(gg + 1) * GB, cc, :],
                                            start=False, stop=stop, skip_group_check=True)
                if cc == PB - 1:
                    last.then_inc(low_used, 1)

            def add_h_tile(k, c, t, stop):
                if c == 0:
                    pe.wait_ge(tile_turned, t + (1 + RAW))
                last = nc.tensor.matmul(h_bank[SEGS[k]][H:P, :], t_quart[:, c * H:(c + 1) * H],
                                        turned[k % TURNED][:, c * BANK:(c + 1) * BANK],
                                        start=False, stop=stop, skip_group_check=True)
                if c == GB - 1:
                    last.then_inc(tile_used, 1)

            def combine_t(j):
                pe.wait_ge(t_copied, j + 1)
                for cc in range(PB):
                    last = nc.tensor.matmul(t_bank[:, PW + cc * H:PW + (cc + 1) * H], t_sum[:, cc * P:(cc + 1) * P],
                                            both[:, :], start=True, stop=True)
                last.then_inc(t_combined, 1)

            def layer0_panel(slot, j, loads, group=None):
                before = (j - 1) * ITEMS

                def add(u):
                    if u >= ITEMS:
                        add_h_low(1 - slot, u - ITEMS, j, False)
                        return
                    add_h(1 - slot, *UNITS[u], before, False)
                    if group is not None and u < TILED // 2 * GB:
                        k = slot * (TILED // 2) + u // GB
                        if slot == 0 and u == 0:
                            pe.wait_ge(t_quartered, group + 1)
                        add_h_tile(k, u % GB, group * TILED + k, False)

                for u, (k, cc) in enumerate(UNITS):
                    if u < ITEMS:
                        turn_blocks(1 - slot, k, cc, before)
                    if u == 0:
                        pe.wait_ge(t_ready, j)
                    if cc == 0:
                        pe.wait_ge(seg_loaded[slot][SEGS[k]], loads)
                    last = add_t(slot, k, cc, PB, seg_done if cc == PB - 1 and k < TILED else None)
                    if u == len(UNITS) - 1:
                        last.then_inc(t_summed, 1)
                    if u > 0:
                        add(u - 1)
                add(len(UNITS) - 1)
                combine_t(j)

            for k in range(NS):
                pe.wait_ge(e_made, k + 1)
                pe.wait_ge(seg_loaded[0][SEGS[k]], DMA)
                last = add_t(0, k, 0, 1)
            last.then_inc(t_summed, 1)
            pe.wait_ge(zeroed, 1)
            for s in SEGS:
                nc.tensor.matmul(h_bank[s][:, :], zeros[:, 0:P], zeros[:, :], start=True, stop=False,
                                 skip_group_check=True)
            combine_t(0)
            layer0_panel(1, 1, DMA)
            with pe.Fori(0, NJ // 2 - 1) as two:
                layer0_panel(0, two * 2 + 2, (two + 2) * DMA, two)
                layer0_panel(1, two * 2 + 3, (two + 2) * DMA, two)

            def turn_h(n, s):
                pe.wait_ge(h_copied, n + 1)
                if n >= 1:
                    pe.wait_ge(y_copied, n)
                for bank, matrix in ((h_bank[s], centre), (t_bank, centre_gamma)):
                    for c in range(GB):
                        last = nc.tensor.matmul(bank[:, c * P:(c + 1) * P], scratch[:, n % 2, c * P:(c + 1) * P],
                                                matrix[:, :], start=True, stop=True)
                last.then_inc(h_turned, 1)

            pe.wait_ge(weights_made, 6)
            pe.wait_ge(t_ready, NJ)
            before = (NJ - 1) * ITEMS
            for u in range(len(UNITS) + 1):
                if u < ITEMS:
                    turn_blocks(1, *UNITS[u], before)
                if u == 0:
                    continue
                k, cc = UNITS[u - 1]
                if k == TILED:
                    add_h_low(1, cc, NJ, cc == PB - 1)
                else:
                    add_h(1, k, cc, before, cc == PB - 1)
                    if u == 1:
                        pe.wait_ge(t_quartered, NG)
                    for c in range(cc * GB // PB, (cc + 1) * GB // PB):
                        add_h_tile(k, c, T1 - TILED + k, c == GB - 1)
                if cc == 0 and k >= 1:
                    turn_h(k - 1, SEGS[k - 1])

            def add_tile(t, place, c, parity, first, last_tile, columns, middle=None):
                pe.wait_ge(tile_turned, t + 1 + RAW)
                for i in range(GB):
                    if i == GB // 2 and middle:
                        middle()
                    last = nc.tensor.matmul(sum_bank[parity][:, :], terms[:, c * GB + i, columns],
                                            turned[place][:, i * BANK:(i + 1) * BANK],
                                            start=(first and i == 0), stop=(last_tile and i == GB - 1),
                                            skip_group_check=True)
                last.then_inc(tile_used, 1)

            def add_tile_halves(t, place, c, parity, first, last_tile, middle=None):
                pe.wait_ge(tile_turned, t + 1 + RAW)
                for i in range(GB):
                    if i == GB // 2 and middle:
                        middle()
                    odd = i % 2
                    last = nc.tensor.matmul(sum_bank[parity][H * odd:H * (odd + 1), :],
                                            terms[:, c * GB + i, 2 * H:3 * H],
                                            turned[place][:, i * BANK:(i + 1) * BANK],
                                            start=(first and i < 2), stop=(last_tile and i >= GB - 2))
                last.then_inc(tile_used, 1)

            def turn_row(n, parity, width):
                pe.wait_ge(row_copied, n + 1)
                for c in range(GB):
                    last = nc.tensor.transpose(back_bank[:, c * width:(c + 1) * width],
                                               scratch[0:width, parity, c * P:(c + 1) * P], ident[0:width, 0:width])
                last.then_inc(row_back, 1)

            def add_diag(g, i):
                last = nc.tensor.matmul(sum_bank[g % 2][H:P, :], terms[:, g * GB + i, H:2 * H],
                                        turned[place1(g, g, 0)][:, i * BANK:(i + 1) * BANK], start=False,
                                        stop=(i == GB - 1), skip_group_check=True)
                if i == GB - 1:
                    last.then_inc(diag_used, 1)

            def turn_u(g):
                pe.wait_ge(u_copied, g + 1)
                for c in range(GB):
                    last = nc.tensor.transpose(back_bank[:, c * P:(c + 1) * P], scratch[:, g % 2, c * P:(c + 1) * P],
                                               ident[:, :])
                last.then_inc(u_back, 1)

            def add_tile_p(t, place, c, parity, first, middle=None, diag=None):
                pe.wait_ge(tile_turned, t + 1 + RAW)
                for i in range(GB):
                    if i == GB // 2 and middle:
                        middle()
                    apart = i % 2 and diag is None
                    last = nc.tensor.matmul(odd_bank[H:P, :] if apart else sum_bank[parity][0:H, :],
                                            terms[:, c * GB + i, 0:H],
                                            turned[place][:, i * BANK:(i + 1) * BANK], start=(first and i == 1),
                                            stop=False, skip_group_check=True)
                    if diag is not None:
                        add_diag(diag, i)
                last.then_inc(tile_used, 1)

            def fold(row, parity):
                pe.wait_ge(odd_copied, row - 1)
                pe.wait_ge(fold_cleared, 1)
                nc.tensor.matmul(sum_bank[parity][0:H, :], both[:, :], squares[:, :], start=False, stop=False,
                                 skip_group_check=True)

            def sweep1_row(row, parity, tile):
                pe.wait_ge(u_copied, row - 1)
                nc.tensor.matmul(sum_bank[parity][:, :], zeros[:, 0:P], zeros[:, :], start=True, stop=False,
                                 skip_group_check=True)
                for k, c in enumerate(DOWN):
                    place = place1(row, c, k)
                    middle = None
                    if k == 0:
                        middle = lambda: turn_q(row - 1)
                    elif k == 4:
                        middle = lambda: turn_u(row - 1)
                    if k == 2:
                        pe.wait_ge(row_written, row)
                        if c < row:
                            for i in range(GB):
                                add_diag(row - 1, i)
                    if c >= row:
                        add_tile_p(tile + k, place, c, parity, k == 0, middle, row - 1 if k == 2 else None)
                        continue
                    if c == row - 1:
                        pe.wait_ge(row_written, row)
                    if c == row - 2 and k == 4:
                        middle = lambda: (turn_u(row - 1), fold(row, parity))
                    elif c == row - 2:
                        middle = lambda: fold(row, parity)
                    add_tile(tile + k, place, c, parity, False, k == NG - 1, slice(0, PH), middle)

            def turn_q(g):
                if g >= 1:
                    pe.wait_ge(u_written, g)
                turn_row(g, g % 2, PH)

            pe.wait_ge(zeroed, 2)
            for n, (g, c) in enumerate(first_rows):
                if n % 4 == 0:
                    pe.wait_ge(normed, n // 4 + 1)
                if n == PAIR - 1:
                    pe.wait_ge(row_written, 1)
                    for i in range(GB):
                        add_diag(0, i)
                middle = {0: lambda: turn_h(NS - 1, SEGS[-1]), PAIR - 2: lambda: turn_q(0),
                          PAIR - 1: lambda: turn_u(0)}.get(n)
                add_tile(T1 + n, place1(g, c, n), c, g, n in (0, 2), n in (PAIR - 3, PAIR - 1), slice(0, PH), middle)
            for g in range(2, NG):
                sweep1_row(g, g % 2, T1 + g * NG)

            turn_q(NG - 1)
            pe.wait_ge(row_written, NG)
            for i in range(GB):
                add_diag(NG - 1, i)
            turn_u(NG - 1)
            t = T2
            for i, g in enumerate(DOWN[1:]):
                for k, c in enumerate(range(NG - 1, g, -1)):
                    if i == 0:
                        pe.wait_ge(u_written, NG)
                    elif c == g + 1:
                        pe.wait_ge(row_written, ROWS1 + i)
                    middle = (lambda: turn_row(ROWS1 + i - 1, 1 - i % 2, H)) if k == 0 and i > 0 else None
                    add_tile(t, late_slots(t - T2)[3], c, i % 2, k == 0, c == g + 1, slice(H, 3 * H), middle)
                    t += 1

            def turn_p(i, g):
                for c in range(GB):
                    last = nc.tensor.transpose(pt_bank[0:H, c * P:(c + 1) * P], terms[:, g * GB + c, 0:H], ident[:, :])
                last.then_inc(pt_turned, 1)

            def output_sums(i, g):
                at = slice(g * BANK, (g + 1) * BANK)
                pe.wait_ge(row_kept, 2 * NG + NG - 1)
                if i:
                    pe.wait_ge(o_copied, i)
                nc.tensor.matmul(o_bank[0:H, :], w_sums1[:, :], sums1[:, at], start=True, stop=False)
                if g < NG - 1:
                    nc.tensor.matmul(o_bank[H:PH, :], w_sums2[:, :], sums2[:, at], start=True, stop=False)

            def output_row(i):
                pe.wait_ge(row_copied, ROWS2 + i + 1)
                nc.tensor.matmul(o_bank[0:H, :], w_sums3[:, :], scratch[:, (ROWS2 + i) % 2, :], start=False, stop=True)\
                    .then_inc(o_summed, 1)

            def output_p(i, g):
                pe.wait_ge(pt_copied, i + 1)
                nc.tensor.matmul(o_bank[H:PH, :], w_p[:, :], p_turned, start=(g == NG - 1), stop=True)\
                    .then_inc(o_summed, 1)

            def turn_output(i):
                pe.wait_ge(o_copied, i + 1)
                if i >= 2:
                    pe.wait_ge(out_taken, i - 1)
                for c in range(GB):
                    last = nc.tensor.transpose(out_bank[i % 2][:, c * P:(c + 1) * P], o_turned[:, c * P:(c + 1) * P],
                                               ident[:, :])
                last.then_inc(out_summed, 1)

            for i, g in enumerate(ROWS3):
                for k in range(g + 1):
                    middle = None
                    if k == 0 and i == 0:
                        middle = lambda: turn_row(ROWS2 - 1, (ROWS2 - 1) % 2, H)
                    elif k == 0:
                        middle = lambda: turn_p(i - 1, ROWS3[i - 1])
                    elif i == NG - 1 and k == g - 1:
                        middle = lambda: turn_p(i, g)
                    elif i == NG - 1 and k == g:
                        middle = lambda: (output_sums(i, g), output_p(i, g))
                    if i == 0 and k == g:
                        pe.wait_ge(row_written, ROWS2)
                    add_tile_halves(t, late_slots(t - T2)[3], g - k, (ROWS2 + i) % 2, k == 0, k == g, middle)
                    t += 1
                    so_far = t - T2 - len(sweep2)
                    if so_far - 2 in END3:
                        turn_output(END3.index(so_far - 2))
                    if k == 0 and i > 0:
                        output_sums(i - 1, ROWS3[i - 1])
                        output_row(i - 1)
                        output_p(i - 1, ROWS3[i - 1])
            output_row(NG - 1)
            turn_output(NG - 1)


_INS = ["x", "adj", "L0_gnn_W_u", "L0_gnn_diag_u", "L0_gnn_par_u", "L0_gnn_W_i", "L0_gnn_diag_i", "L0_gnn_par_i",
        "L0_gnn_ln_gamma", "L0_gnn_ln_beta", "L1_gnn_weight", "L1_gnn_bias"]


def kernel(**inputs):
    import numpy as _np
    import concourse.bacc as _bacc
    from concourse.bass_utils import run_bass_kernel_spmd as _run

    nc = _bacc.Bacc("TRN2", target_bir_lowering=False, num_devices=1)
    arrays, args = {}, []
    for name in _INS:
        a = _np.ascontiguousarray(inputs[name])
        arrays[f"in_{name}"] = a
        args.append(nc.dram_tensor(f"in_{name}", a.shape, mybir.dt.from_np(a.dtype), kind="ExternalInput").ap())
    shape = inputs["x"].shape
    args.append(nc.dram_tensor("out_0", shape, F32, kind="ExternalOutput").ap())
    resnorm_chebyshev(nc, *args)
    r = _run(nc, [arrays], core_ids=[0])
    return r.results[0]["out_0"]
```
